# Optimizing a Trainium2 kernel written in Bass

```python
import numpy as np
import jax
import jax.numpy as jnp

def _softmax(x, axis=-1):
    return jax.nn.softmax(x, axis=axis)

def _gelu(x):
    return jax.nn.gelu(x, approximate=True)

def _silu(x):
    return jax.nn.silu(x)

def _sigmoid(x):
    return jax.nn.sigmoid(x)

def _layernorm(x, axis=-1, eps=1e-05):
    m = jnp.mean(x, axis=axis, keepdims=True)
    v = jnp.var(x, axis=axis, keepdims=True)
    return (x - m) / jnp.sqrt(v + eps)

def _scatter_add(tgt, idx, src, axis=0):
    return tgt.at[idx].add(src)

def _segment_sum(src, seg, n):
    return jax.ops.segment_sum(src, seg, n)
kernel_name = 'mk_decoder_preln_d1_seqx_r8_3be545'

def setup_inputs(seed: int=0):
    np.random.seed(seed)
    _w = jnp.asarray

    def _rec_inputs():
        import jax
        import jax.numpy as jnp
        _rk = jax.random.key(seed)
        x = -0.000125 + 0.9999 * jax.random.normal(jax.random.fold_in(_rk, 1), (4, 256, 256), jnp.float32)
        _lenS = 256 - jax.random.randint(jax.random.fold_in(_rk, 7), (4,), 0, max(1, 256 // 4) + 1, jnp.int32)
        _lenS2 = 256 - jax.random.randint(jax.random.fold_in(_rk, 8), (4,), 0, max(1, 256 // 4) + 1, jnp.int32)
        itok_BxS_13_99985 = jax.random.randint(jax.random.fold_in(_rk, 11), (4, 256), 13, 99986, jnp.int32)
        _ctx_2048P = jax.random.normal(jax.random.fold_in(_rk, 12), (4, 16, 256), jnp.float32)
        _ctx_2048c = jax.random.dirichlet(jax.random.fold_in(_rk, 512), 0.3 * jnp.ones((16,), jnp.float32), (4, 256))
        _ctx_2048t = jnp.einsum('bsk,bkd->bsd', _ctx_2048c, _ctx_2048P)
        _ctx_2048t = _ctx_2048t * jax.lax.rsqrt(jnp.mean(jnp.square(_ctx_2048t)) + 1e-12) * 0.953939
        ctx_2048 = 6.82029e-06 + 0.0200006 * (_ctx_2048t + 0.3 * jax.random.normal(jax.random.fold_in(_rk, 612), (4, 256, 256), jnp.float32))
        return (x, itok_BxS_13_99985, ctx_2048)
    x, itok_BxS_13_99985, ctx_2048 = _rec_inputs()

    def _L0_attn_setup():
        import jax, jax.numpy as jnp
        import numpy as np
        import math
        N_HEAD = 16
        LAYER = 1
        LAMBDA_INIT = 0.8 - 0.6 * math.exp(-0.3 * (LAYER - 1))
        key = jax.random.key(seed)
        ks = jax.random.split(key, 7)
        B, T, E = (2, 256, 256)
        s = 0.02
        return {'x': jax.random.normal(ks[0], (B, T, E), dtype=jnp.float32), 'W_attn': jax.random.normal(ks[1], (E, 3 * E), dtype=jnp.float32) * s, 'W_proj': jax.random.normal(ks[2], (E, E), dtype=jnp.float32) * s, 'lambda_q1': jax.random.normal(ks[3], (E,), dtype=jnp.float32) * 0.1, 'lambda_k1': jax.random.normal(ks[4], (E,), dtype=jnp.float32) * 0.1, 'lambda_q2': jax.random.normal(ks[5], (E,), dtype=jnp.float32) * 0.1, 'lambda_k2': jax.random.normal(ks[6], (E,), dtype=jnp.float32) * 0.1}
    _L0_attn_all = _L0_attn_setup()
    _L0_attn_in = {k: v for k, v in _L0_attn_all.items() if k in ('W_attn', 'W_proj', 'lambda_q1', 'lambda_k1', 'lambda_q2', 'lambda_k2')}
    del _L0_attn_all

    def _L0_xattn_setup():
        import jax, jax.numpy as jnp
        import numpy as np
        B, S, D = (4, 512, 256)
        E = 4
        F = 1024 // E
        VOCAB = 12500
        key = jax.random.key(seed)
        k1, k2, k3, k4, k5 = jax.random.split(key, 5)
        hidden_states = jax.random.normal(k1, (B, S, D), dtype=jnp.float32)
        token_ids = jax.random.randint(k2, (B, S), 0, VOCAB, dtype=jnp.int64)
        Wg = jax.random.normal(k3, (E, F, D), dtype=jnp.float32) * 0.02
        Wu = jax.random.normal(k4, (E, F, D), dtype=jnp.float32) * 0.02
        Wd = jax.random.normal(k5, (E, D, F), dtype=jnp.float32) * 0.02
        return {'hidden_states': hidden_states, 'token_ids': token_ids, 'Wg': Wg, 'Wu': Wu, 'Wd': Wd}
    _L0_xattn_all = _L0_xattn_setup()
    _L0_xattn_in = {k: v for k, v in _L0_xattn_all.items() if k in ()}
    del _L0_xattn_all

    def _L0_ffn_setup():
        import jax, jax.numpy as jnp
        import numpy as np
        B, S, H = (4, 256, 256)
        INTER = 512
        E = 8
        TOPK = 2
        SHARED_I = INTER * 2

        def moe_forward(hidden_states, router_w, w1, w2, w_gate, w_up, w_down):
            b, s, h = hidden_states.shape
            x = hidden_states.reshape(-1, h)
            T = x.shape[0]
            logits = x @ router_w
            top_logits, top_indices = jax.lax.top_k(logits, TOPK)
            scores = jax.nn.softmax(top_logits, axis=-1)
            flat_idx = top_indices.reshape(-1)
            sorted_pos = jnp.argsort(flat_idx, stable=True)
            permuted = x[sorted_pos // TOPK]
            expert_ids = flat_idx[sorted_pos]
            out = jnp.zeros((T * TOPK, h), x.dtype)
            for e in range(E):
                mask = (expert_ids == e)[:, None]
                f1 = permuted * mask @ w1[e]
                g, u = jnp.split(f1, 2, axis=-1)
                act = jax.nn.silu(g) * u
                out = out + jnp.where(mask, act @ w2[e], 0.0)
            unperm = jnp.zeros_like(out).at[sorted_pos].set(out)
            combined = (unperm.reshape(T, TOPK, h) * scores[..., None]).sum(axis=1)
            shared = jax.nn.silu(x @ w_gate) * (x @ w_up) @ w_down
            return (combined + shared).reshape(b, s, h)
        key = jax.random.key(seed)
        ks = jax.random.split(key, 7)
        s = 0.02
        return {'hidden_states': jax.random.normal(ks[0], (B, S, H), jnp.float32), 'router_w': jax.random.normal(ks[1], (H, E), jnp.float32) * s, 'w1': jax.random.normal(ks[2], (E, H, 2 * INTER), jnp.float32) * s, 'w2': jax.random.normal(ks[3], (E, INTER, H), jnp.float32) * s, 'w_gate': jax.random.normal(ks[4], (H, SHARED_I), jnp.float32) * s, 'w_up': jax.random.normal(ks[5], (H, SHARED_I), jnp.float32) * s, 'w_down': jax.random.normal(ks[6], (SHARED_I, H), jnp.float32) * s}
    _L0_ffn_all = _L0_ffn_setup()
    _L0_ffn_in = {k: v for k, v in _L0_ffn_all.items() if k in ('router_w', 'w1', 'w2', 'w_gate', 'w_up', 'w_down')}
    del _L0_ffn_all
    return {'x': x, 'itok_BxS_13_99985': itok_BxS_13_99985, 'ctx_2048': ctx_2048, 'L0_attn_W_attn': _L0_attn_in['W_attn'], 'L0_attn_W_proj': _L0_attn_in['W_proj'], 'L0_attn_lambda_q1': _L0_attn_in['lambda_q1'], 'L0_attn_lambda_k1': _L0_attn_in['lambda_k1'], 'L0_attn_lambda_q2': _L0_attn_in['lambda_q2'], 'L0_attn_lambda_k2': _L0_attn_in['lambda_k2'], 'L0_ffn_router_w': _L0_ffn_in['router_w'], 'L0_ffn_w1': _L0_ffn_in['w1'], 'L0_ffn_w2': _L0_ffn_in['w2'], 'L0_ffn_w_gate': _L0_ffn_in['w_gate'], 'L0_ffn_w_up': _L0_ffn_in['w_up'], 'L0_ffn_w_down': _L0_ffn_in['w_down']}

def reference(x, itok_BxS_13_99985, ctx_2048, L0_attn_W_attn, L0_attn_W_proj, L0_attn_lambda_q1, L0_attn_lambda_k1, L0_attn_lambda_q2, L0_attn_lambda_k2, L0_ffn_router_w, L0_ffn_w1, L0_ffn_w2, L0_ffn_w_gate, L0_ffn_w_up, L0_ffn_w_down):
    import jax
    import jax.numpy as jnp

    def _L0_attn_ref(x, W_attn, W_proj, lambda_q1, lambda_k1, lambda_q2, lambda_k2):
        import jax, jax.numpy as jnp
        import numpy as np
        import math
        N_HEAD = 16
        LAYER = 1
        LAMBDA_INIT = 0.8 - 0.6 * math.exp(-0.3 * (LAYER - 1))
        B, T, E = x.shape
        C = E // 2
        H = N_HEAD
        hd = E // H // 2
        scale = hd ** (-0.5)
        qkv = x @ W_attn
        q1 = qkv[..., 0 * C:1 * C].reshape(B, T, H, hd)
        k1 = qkv[..., 1 * C:2 * C].reshape(B, T, H, hd)
        q2 = qkv[..., 2 * C:3 * C].reshape(B, T, H, hd)
        k2 = qkv[..., 3 * C:4 * C].reshape(B, T, H, hd)
        v = qkv[..., 4 * C:6 * C].reshape(B, T, H, 2 * hd)
        lam = jnp.exp(jnp.dot(lambda_q1, lambda_k1)) - jnp.exp(jnp.dot(lambda_q2, lambda_k2)) + LAMBDA_INIT
        attn1 = jnp.einsum('bthd,bshd->bhts', q1, k1) * scale
        attn2 = jnp.einsum('bthd,bshd->bhts', q2, k2) * scale
        score = jax.nn.softmax(attn1 - lam * attn2, axis=-1)
        out = jnp.einsum('bhts,bshd->bthd', score, v)
        out = (1.0 - LAMBDA_INIT) * out.reshape(B, T, E)
        return out @ W_proj

    def _L0_xattn_ref(hidden_states, token_ids, Wg, Wu, Wd):
        import jax, jax.numpy as jnp
        import numpy as np
        B, S, D = (4, 512, 256)
        E = 4
        F = 1024 // E
        VOCAB = 12500
        tokens_per_expert = VOCAB // E
        tid = jnp.clip(token_ids, 0, VOCAB - 1)
        expert_ids = jnp.minimum(tid // tokens_per_expert, E - 1)
        out = jnp.zeros_like(hidden_states)
        for e in range(E):
            g = jax.nn.silu(jnp.einsum('bsd,fd->bsf', hidden_states, Wg[e]))
            u = jnp.einsum('bsd,fd->bsf', hidden_states, Wu[e])
            y = jnp.einsum('bsf,df->bsd', g * u, Wd[e])
            out = jnp.where((expert_ids == e)[..., None], y, out)
        return out

    def _L0_ffn_ref(hidden_states, router_w, w1, w2, w_gate, w_up, w_down):
        import jax, jax.numpy as jnp
        import numpy as np
        B, S, H = (4, 256, 256)
        INTER = 512
        E = 8
        TOPK = 2
        SHARED_I = INTER * 2

        def moe_forward(hidden_states, router_w, w1, w2, w_gate, w_up, w_down):
            b, s, h = hidden_states.shape
            x = hidden_states.reshape(-1, h)
            T = x.shape[0]
            logits = x @ router_w
            top_logits, top_indices = jax.lax.top_k(logits, TOPK)
            scores = jax.nn.softmax(top_logits, axis=-1)
            flat_idx = top_indices.reshape(-1)
            sorted_pos = jnp.argsort(flat_idx, stable=True)
            permuted = x[sorted_pos // TOPK]
            expert_ids = flat_idx[sorted_pos]
            out = jnp.zeros((T * TOPK, h), x.dtype)
            for e in range(E):
                mask = (expert_ids == e)[:, None]
                f1 = permuted * mask @ w1[e]
                g, u = jnp.split(f1, 2, axis=-1)
                act = jax.nn.silu(g) * u
                out = out + jnp.where(mask, act @ w2[e], 0.0)
            unperm = jnp.zeros_like(out).at[sorted_pos].set(out)
            combined = (unperm.reshape(T, TOPK, h) * scores[..., None]).sum(axis=1)
            shared = jax.nn.silu(x @ w_gate) * (x @ w_up) @ w_down
            return (combined + shared).reshape(b, s, h)
        return moe_forward(hidden_states, router_w, w1, w2, w_gate, w_up, w_down)
    x = x + _L0_attn_ref(_layernorm(x, axis=-1), L0_attn_W_attn, L0_attn_W_proj, L0_attn_lambda_q1, L0_attn_lambda_k1, L0_attn_lambda_q2, L0_attn_lambda_k2)
    x = x + _L0_xattn_ref(_layernorm(x, axis=-1), itok_BxS_13_99985, ctx_2048, ctx_2048, ctx_2048)
    x = x + _L0_ffn_ref(_layernorm(x, axis=-1), L0_ffn_router_w, L0_ffn_w1, L0_ffn_w2, L0_ffn_w_gate, L0_ffn_w_up, L0_ffn_w_down)
    return x

_drawn_inputs = setup_inputs


def setup_inputs(seed=0):
    import zlib

    import numpy as np

    out = dict(_drawn_inputs(seed))
    spreads = {}
    factors = {'L0_attn_W_attn': 8.0,
     'L0_attn_W_proj': 8.0,
     'L0_attn_lambda_q1': 8.0,
     'L0_attn_lambda_k1': 8.0,
     'L0_attn_lambda_q2': 64.0,
     'L0_attn_lambda_k2': 64.0,
     'L0_ffn_router_w': 3.811,
     'L0_ffn_w1': 3.318,
     'L0_ffn_w2': 3.318,
     'ctx_2048': 6.615,
     'L0_ffn_w_gate': 8.0,
     'L0_ffn_w_up': 8.0,
     'L0_ffn_w_down': 8.0}
    for name, (base, spread) in spreads.items():
        noise = np.random.default_rng([zlib.crc32(name.encode()), seed]).standard_normal(out[name].shape)
        drawn = base * np.exp(spread * noise) if base else spread * noise
        out[name] = jnp.asarray(drawn.astype(out[name].dtype))
    for name, factor in factors.items():
        out[name] = (out[name] * factor).astype(out[name].dtype)
    return out
```

```python
from contextlib import ExitStack

import numpy as np

import concourse.bass as bass
from concourse import mybir

F32 = mybir.dt.float32
BF16 = mybir.dt.bfloat16
I32 = mybir.dt.int32
U32 = mybir.dt.uint32
ALU = mybir.AluOpType
ACT = mybir.ActivationFunctionType
AXX = mybir.AxisListType.X

P = 128
B, S, D = 4, 256, 256
T = B * S
TT = T // P
TB = S // P
HALF = T // 2
TH = HALF // P
KD = D // P
H = 16
HD = D // H
HP = 32
Q4 = 4
NQ = H // Q4
LAMBDA_INIT = 0.2
SCALE = float(HD // 2) ** -0.5
EPS = 1e-5
Q_PARTS = (0, 0, 1, 0, 2, 1)
K_PARTS = (0, 1, 0, 2, 0, 1)
NT = len(Q_PARTS)
KS_ROWS = NT * HD
KA_ROWS = KS_ROWS + 3
XE = 4
VOCAB = 12500
PER_X = VOCAB // XE
E = 8
INTER = 512
SHARED = 1024
MAGIC = float(0x5F3759DF)

S_IN_SLOT = (3, 3, 3, 3, 3, 1, 0, 0)


def decoder_layer(nc, x, ids, ctxT, w_qk, w_v, w_proj, lam_vecs, router_w, w1, w2, w_gate, w_up, w_down,
                  ident_c, sel_c, coef_c, iota_c, out):
    with ExitStack() as ctx:
        def sb(name, shape, dt=F32):
            return ctx.enter_context(nc.sbuf_tensor(name, shape, dt))

        def sem(name):
            return ctx.enter_context(nc.semaphore(name))

        xs = sb("xs", [P, TT, D])
        hn = sb("hn", [P, TT, D])
        hT = sb("hT", [P, KD, T])
        st6 = sb("st6", [P, TT, 6])
        mv = sb("mv", [P, TT, 2])
        nw = sb("nw", [P, 6, TT])
        wqk = sb("wqk", [P, KD, 2 * D])
        wv = sb("wv", [P, KD, D])
        wp = sb("wp", [P, NQ, D])
        ident = sb("ident", [P, P])
        sel = sb("sel", [P, P])
        coefc = sb("coefc", [P, 2])
        lamv = sb("lamv", [P, 4, D])
        lam = sb("lam", [P, 8])
        coef = sb("coef", [P, 1])
        fq = sb("fq", [P, 2, HALF])
        tq = sb("tq", [P, 2, HALF])
        big = sb("big", [P, 24576])
        qst = big[:, 0:8192].bitcast(BF16).rearrange("p (h t) -> p h t", h=H)
        kst = big[:, 8192:16384].bitcast(BF16).rearrange("p (h t) -> p h t", h=H)
        vall = big[:, 16384:18432].rearrange("p (t h d) -> p t h d", t=TT, h=H)
        vaug = big[:, 18432:19456].rearrange("p (t h d) -> p t h d", t=TB, h=H)
        pt = big[:, 19456:21504].rearrange("p (s n) -> p s n", s=2)
        osb = big[:, 21504:22528].rearrange("p (q t) -> p q t", q=NQ)
        onm = big[:, 22528:23552].rearrange("p (q t) -> p q t", q=NQ)
        rcp = big[:, 23552:23808]
        mid = sb("mid", [P, 6144])
        parts = mid[:, :].bitcast(BF16).rearrange("p (w j b t) -> p w j b t", w=2, j=3, b=2)
        rmax = sb("rmax", [P, TB, H])
        nmf = sb("nmf", [2 * H, 2, P])
        nmp = sb("nmp", [2 * H, 3, P], BF16)
        ct = sb("ct", [P, XE, KD, D])
        idb = sb("idb", [P, T], I32)
        idf = sb("idf", [P, T])
        xmask = sb("xmask", [P, XE, T], BF16)
        xge = sb("xge", [P, 2, T], BF16)
        aT = mid[:, 0:4096].rearrange("p (f t) -> p f t", f=8)
        sg = mid[:, 4096:5120].rearrange("p (s t) -> p s t", s=2)
        pm = mid[:, 5120:6144].rearrange("p (s t) -> p s t", s=2)
        rw = sb("rw", [P, KD, E])
        iota = sb("iota", [P, E])
        lg = sb("lg", [P, TT, E])
        mx8 = sb("mx8", [P, TT, 8])
        ix8 = sb("ix8", [P, TT, 8], U32)
        ixf = sb("ixf", [P, TT, 2])
        oh = sb("oh", [P, 2, TT, E])
        gw = sb("gw", [P, 4, TT])
        cw = sb("cw", [P, TT, E])
        wgu = big[:, 0:4096].rearrange("p (s k f) -> p s k f", s=4, k=KD)
        wdn = big[:, 4096:6144].rearrange("p (s k n) -> p s k n", s=2, k=INTER // P)

        ps_s = [ctx.enter_context(nc.psum_tensor(f"ps_s{i}", [P, 512], F32)) for i in range(2)]
        ps_t = [ctx.enter_context(nc.psum_tensor(f"ps_t{i}", [P, 1024], F32)) for i in range(2)]
        ps_o = ctx.enter_context(nc.psum_tensor("ps_o", [P, 512], F32))
        ps_m = ctx.enter_context(nc.psum_tensor("ps_m", [P, 512], F32))

        qk_dram = nc.dram_tensor("qk_parts", (2, 3, KD, P, T), BF16, kind="Internal").ap()
        mx_dram = nc.dram_tensor("mx_parts", (3, TB, H, P), BF16, kind="Internal").ap()

        ld_x = [sem(f"ld_x{i}") for i in range(2)]
        ld_c = sem("ld_c")
        ld_ids = sem("ld_ids")
        ld_wqk = sem("ld_wqk")
        ld_wv = sem("ld_wv")
        ld_wp = sem("ld_wp")
        ld_ct = sem("ld_ct")
        ld_rw = sem("ld_rw")
        s_const = sem("s_const")
        dve_step = sem("dve_step")
        act_step = sem("act_step")
        coef_ok = sem("coef_ok")
        lam_dot = sem("lam_dot")
        lam_exp = sem("lam_exp")
        h_ready = sem("h_ready")
        hT_ps = sem("hT_ps")
        hT_sb = sem("hT_sb")
        qk_ps = sem("qk_ps")
        qk_f = sem("qk_f")
        qk_h = sem("qk_h")
        qk_t = sem("qk_t")
        qk_m = sem("qk_m")
        qk_l = sem("qk_l")
        qk_out = [sem(f"qk_out{i}") for i in range(2)]
        qk_in = [sem(f"qk_in{i}") for i in range(2)]
        v_ps = sem("v_ps")
        v_sb = sem("v_sb")
        s_ready = sem("s_ready")
        s_used = sem("s_used")
        rm_T = sem("rm_T")
        nm_ready = sem("nm_ready")
        aug_out = sem("aug_out")
        aug_in = sem("aug_in")
        t_ready = sem("t_ready")
        p_ready = sem("p_ready")
        pv_done = sem("pv_done")
        o_evac = sem("o_evac")
        bc_ready = sem("bc_ready")
        m_used = sem("m_used")
        on_ready = sem("on_ready")
        pr_ready = sem("pr_ready")
        vaug_ok = sem("vaug_ok")
        x1_ok = sem("x1_ok")
        mask_ok = sem("mask_ok")
        pool_step = sem("pool_step")
        xp_ps = sem("xp_ps")
        xp_sg = sem("xp_sg")
        xp_pm = sem("xp_pm")
        xa_ok = sem("xa_ok")
        xy_ps = sem("xy_ps")
        x2_ok = sem("x2_ok")
        lg_ps = sem("lg_ps")
        lg_sb = sem("lg_sb")
        gd_ok = sem("gd_ok")
        ge_ok = sem("ge_ok")
        cw_ok = sem("cw_ok")
        gu_ps = sem("gu_ps")
        gu_sg = sem("gu_sg")
        ga_ok = sem("ga_ok")
        gy_ps = sem("gy_ps")
        gy_ok = sem("gy_ok")
        ld_e = [sem(f"ld_e{i}") for i in range(2)]
        s_out = sem("s_out")

        x_rows = x.rearrange("b (s p) d -> p (b s) d", p=P)
        out_rows = out.rearrange("b (s p) d -> p (b s) d", p=P)

        JOBS = [(w1[e, :, 0:INTER], w1[e, :, INTER:2 * INTER], w2[e, :, :], e) for e in range(E)]
        JOBS += [(w_gate[:, c * INTER:(c + 1) * INTER], w_up[:, c * INTER:(c + 1) * INTER],
                  w_down[c * INTER:(c + 1) * INTER, :], None) for c in range(SHARED // INTER)]
        NJ = len(JOBS)
        FB = INTER // P

        block = ctx.enter_context(nc.Block())

        class Steps:

            def __init__(self, eng, s):
                self.eng, self.s, self.n, self.off = eng, s, 0, None

            def done(self, ins):
                self.n += 1
                ins.then_inc(self.s, 1)

            def wait(self):
                self.eng.wait_ge(self.s, self.n if self.off is None else self.off + self.n)

        @block.sync
        def _(sp):
            for hf in range(2):
                sp.dma_start(xs[:, hf * TH:(hf + 1) * TH, :], x_rows[:, hf * TH:(hf + 1) * TH, :]).then_inc(ld_x[hf], 16)
            sp.dma_start(lamv[:], lam_vecs.partition_broadcast(P)).then_inc(ld_c, 16)
            sp.dma_start(coefc[:], coef_c).then_inc(ld_c, 16)
            sp.dma_start(iota[:], iota_c).then_inc(ld_c, 16)
            sp.dma_start(sel[:], sel_c).then_inc(ld_c, 16)
            sp.dma_start(wp[:], w_proj).then_inc(ld_wp, 16)
            sp.dma_start(idb[:], ids.partition_broadcast(P)).then_inc(ld_ids, 16)
            sp.dma_start(rw[:], router_w.rearrange("(k p) e -> p k e", p=P)).then_inc(ld_rw, 16)
            for hf in range(2):
                tok = slice(hf * HALF, (hf + 1) * HALF)
                for w in range(2):
                    sp.wait_ge(qk_h, 4 * hf + 2 * w + 2)
                    sp.wait_ge(qk_m, 4 * hf + 2 * w + 2)
                    sp.wait_ge(qk_l, 4 * hf + 2 * w + 2)
                    for j in range(3):
                        sp.dma_start(qk_dram[w, j, :, :, tok].rearrange("b p t -> p b t"),
                                     parts[:, w, j, :, tok]).then_inc(qk_out[hf], 16)
                sp.wait_ge(qk_out[hf], 96)
                for dst, w, of in ((qst, 0, Q_PARTS), (kst, 1, K_PARTS)):
                    for j, part in enumerate(of):
                        src = qk_dram[w, part, :, :, tok].rearrange("b (h d) t -> d (b h) t", d=HD)
                        sp.dma_start(dst[HD * j:HD * (j + 1), :, tok], src).then_inc(qk_in[hf], 16)
                if hf == 0:
                    sp.dma_start(ct[:], ctxT).then_inc(ld_ct, 16)

            def aug(b):
                sp.wait_ge(nm_ready, b + 1)
                sp.dma_start(mx_dram.rearrange("j t h n -> (t h) j n"), nmp[:, :, :]).then_inc(aug_out, 16)
                sp.wait_ge(aug_out, 16 * b + 16)
                for tt in range(TB):
                    sp.dma_start(qst[KS_ROWS:KA_ROWS, :, bass.ds(b * S + tt * P, P)],
                                 mx_dram[:, tt, :, :]).then_inc(aug_in, 16)

            aug(0)
            with sp.Fori(1, B) as b:
                aug(b)
            sp.wait_ge(pr_ready, B + 1)
            for n in range(2 * NJ):
                g, u, d, _ = JOBS[n % NJ]
                if n >= 2:
                    sp.wait_ge(gy_ps, 4 * (n - 1))
                s = n % 2
                sp.dma_start(wgu[:, 2 * s, :, :], g.rearrange("(k p) f -> p k f", p=P)).then_inc(ld_e[s], 16)
                sp.dma_start(wgu[:, 2 * s + 1, :, :], u.rearrange("(k p) f -> p k f", p=P)).then_inc(ld_e[s], 16)
                sp.dma_start(wdn[:, s, 0:FB, :], d.rearrange("(k p) n -> p k n", p=P)).then_inc(ld_e[s], 16)
            for hf in range(2):
                sp.wait_ge(gy_ok, 4 * NJ * (hf + 1))
                sp.dma_start(out_rows[:, hf * TH:(hf + 1) * TH, :], xs[:, hf * TH:(hf + 1) * TH, :]).then_inc(s_out, 16)
            sp.wait_ge(s_out, 32)

        @block.gpsimd
        def _(pool):
            pool.memset(vaug[:, :, :, :], 0.0).then_inc(pool_step, 1)
            pool.wait_ge(pool_step, 1)
            pool.memset(vaug[:, :, :, HD:HD + 1], 1.0).then_inc(s_const, 1)
            pool.wait_ge(s_const, 1)
            pool.memset(kst[KS_ROWS:KA_ROWS, :, :], 1.0).then_inc(s_const, 1)
            pool.wait_ge(s_const, 2)
            steps = 1
            for hf in range(2):
                for n in range(4 * hf, 4 * hf + 4):
                    w, blk = (n % 4) // 2, n % 2
                    pool.wait_ge(qk_t, n + 1)
                    pool.tensor_copy(parts[:, w, 1, blk, hf * HALF:(hf + 1) * HALF], tq[:, n % 2, :]).then_inc(qk_m, 1)
            pool.wait_ge(ld_ids, 16)
            pool.tensor_copy(idf[:], idb[:]).then_inc(pool_step, 1)
            steps += 1
            pool.wait_ge(pool_step, steps)
            for e in range(1, XE):
                a, c = (e - 1) % 2, e % 2
                if e == 1:
                    pool.memset(xge[:, 0, :], 1.0).then_inc(pool_step, 1)
                    steps += 1
                pool.tensor_scalar(xge[:, c, :], idf[:], float(PER_X * e), None, ALU.is_ge).then_inc(pool_step, 1)
                steps += 1
                pool.wait_ge(pool_step, steps)
                pool.tensor_tensor(xmask[:, e - 1, :], xge[:, a, :], xge[:, c, :], ALU.subtract).then_inc(pool_step, 1)
                steps += 1
                pool.wait_ge(pool_step, steps)
                if e == XE - 1:
                    pool.tensor_copy(xmask[:, e, :], xge[:, c, :]).then_inc(mask_ok, 1)

            def vcopy(b, src):
                pool.wait_ge(pv_done, 8 * b + 2)
                pool.tensor_copy(vaug[:, :, :, 0:HD], src).then_inc(vaug_ok, 1)

            pool.wait_ge(v_sb, 4)
            pool.wait_ge(s_const, 2)
            with pool.Fori(0, B) as b:
                vcopy(b, vall[:, bass.ds(b * TB, TB), :, :])
            pool.wait_ge(mask_ok, 1)
            for n in range(2 * XE * KD):
                hf, e, fb = n // 8, (n % 8) // 2, n % 2
                pool.wait_ge(xp_pm, n + 1)
                if hf == 1:
                    pool.wait_ge(xy_ps, TH)
                pool.tensor_tensor(aT[:, n % 8, :], pm[:, n % 2, :], xmask[:, e, hf * HALF:(hf + 1) * HALF],
                                   ALU.mult).then_inc(xa_ok, 1)

        @block.scalar
        def _(act):
            act.dma_start(ident[:], ident_c).then_inc(ld_wqk, 16)
            act.dma_start(wqk[:], w_qk).then_inc(ld_wqk, 16)
            act.dma_start(wv[:], w_v).then_inc(ld_wv, 16)
            act.sem_inc(p_ready, 2)
            act.sem_inc(o_evac, 1)
            act.wait_ge(lam_dot, 2)
            act.activation(lam[:, 2:4], lam[:, 0:2], ACT.Exp).then_inc(lam_exp, 1)

            def evac_hT(stage, hf, banks):
                for k in range(KD):
                    n = 4 * stage + 2 * hf + k + 1
                    act.wait_ge(hT_ps, n)
                    act.activation(hT[:, k, hf * HALF:(hf + 1) * HALF], banks[k], ACT.Copy).then_inc(hT_sb, 1)

            for hf in range(2):
                evac_hT(0, hf, (ps_s[0][:], ps_s[1][:]))
                if hf == 0:
                    act.wait_ge(coef_ok, 1)
                for n in range(4 * hf, 4 * hf + 4):
                    w, blk = (n % 4) // 2, n % 2
                    bank = ps_t[(n % 4) // 2][:, (n % 2) * 512:(n % 2 + 1) * 512]
                    act.wait_ge(qk_ps, n + 1)
                    if n >= 2:
                        act.wait_ge(qk_t, n - 1)
                    sc = coef[:, 0:1] if w == 0 else 1.0
                    act.activation(fq[:, n % 2, :], bank, ACT.Copy, scale=sc).then_inc(qk_f, 1)
                    act.activation(parts[:, w, 0, blk, hf * HALF:(hf + 1) * HALF], bank, ACT.Copy, scale=sc).then_inc(qk_h, 1)

            def batch(b):
                for i in range(8):
                    act.wait_ge(t_ready, 8 * b + i + 1)
                    act.wait_ge(pv_done, 8 * b + i + 1)
                    act.activation(pt[:, i % 2, :], ps_t[i % 2][:], ACT.Exp).then_inc(p_ready, 1)
                    if (i % 2 == 0 and i > 0) or i == 7:
                        q = i // 2 - 1 if i < 7 else NQ - 1
                        act.wait_ge(pv_done, 8 * b + 2 * q + 4)
                        act.wait_ge(on_ready, 4 * b + q + 1)
                        act.activation(osb[:, q, :], ps_o[:, 0:S], ACT.Copy).then_inc(o_evac, 1)

            with act.Fori(0, B) as b:
                batch(b)

            LB = (ps_o[:], ps_m[:])
            for hf in range(2):
                evac_hT(1, hf, LB)
            for n in range(2 * XE * KD):
                act.wait_ge(xp_ps, n + 1)
                if n >= 2:
                    act.wait_ge(xp_pm, n - 1)
                act.activation(sg[:, n % 2, :], ps_t[(n % 4) // 2][:, (n % 2) * 512:(n % 2 + 1) * 512],
                               ACT.Silu).then_inc(xp_sg, 1)
            for hf in range(2):
                evac_hT(2, hf, LB)
            act.wait_ge(gd_ok, 1)
            act.activation(gw[:, 1, :], gw[:, 0, :], ACT.Exp).then_inc(ge_ok, 1)
            for n in range(2 * NJ * FB):
                act.wait_ge(gu_ps, n + 1)
                if n >= 2:
                    act.wait_ge(ga_ok, n - 1)
                act.activation(sg[:, n % 2, :], ps_t[n % 2][:, 0:512], ACT.Silu).then_inc(gu_sg, 1)

        @block.vector
        def _(dve):
            mine = Steps(dve, dve_step)
            dve.sem_inc(s_used, 2)
            dve.sem_inc(on_ready, NQ)

            def layernorm(stage, hf, arrived):
                t0 = hf * TH
                for t in range(t0, t0 + TH):
                    arrived(t)
                    mine.done(dve.bn_stats(st6[:, t, :], xs[:, t, :]))
                mine.wait()
                for t in range(t0, t0 + TH):
                    mine.done(dve.bn_aggr(mv[:, t, :], st6[:, t, :]))
                mine.wait()
                ts = slice(t0, t0 + TH)
                var, half, y, a, c = (nw[:, i, ts] for i in range(5))
                mine.done(dve.tensor_scalar(var, mv[:, ts, 1], EPS, None, ALU.add))
                mine.wait()
                mine.done(dve.tensor_scalar(half.bitcast(I32), var.bitcast(I32), 1, None, ALU.logical_shift_right))
                mine.wait()
                mine.done(dve.tensor_scalar(y.bitcast(I32), half.bitcast(I32), -1.0, MAGIC, ALU.mult, ALU.add))
                mine.wait()
                for _ in range(4):
                    mine.done(dve.tensor_tensor(a, y, y, ALU.mult))
                    mine.wait()
                    mine.done(dve.scalar_tensor_tensor(out=c, in0=a, scalar=-0.5, in1=var, op0=ALU.mult, op1=ALU.mult))
                    mine.wait()
                    mine.done(dve.scalar_tensor_tensor(out=y, in0=c, scalar=1.5, in1=y, op0=ALU.add, op1=ALU.mult))
                    mine.wait()
                for t in range(t0, t0 + TH):
                    dve.tensor_scalar(hn[:, t, :], xs[:, t, :], mv[:, t, 0:1], nw[:, 2, t:t + 1],
                                      ALU.subtract, ALU.mult).then_inc(h_ready, 1)

            layernorm(0, 0, lambda t: dve.wait_ge(ld_x[0], 16))
            dve.wait_ge(ld_c, 64)
            for i in range(2):
                dve.tensor_tensor_reduce(lamv[:, 2 * i, :], lamv[:, 2 * i, :], lamv[:, 2 * i + 1, :], 1.0, 0.0,
                                         ALU.mult, ALU.add, lam[:, i:i + 1]).then_inc(lam_dot, 1)
            dve.wait_ge(lam_exp, 1)
            mine.done(dve.tensor_tensor(lam[:, 4:5], lam[:, 2:3], lam[:, 3:4], ALU.subtract))
            mine.wait()
            mine.done(dve.tensor_scalar(lam[:, 5:6], lam[:, 4:5], LAMBDA_INIT, None, ALU.add))
            mine.wait()
            dve.tensor_scalar(coef[:], coefc[:, 1:2], lam[:, 5:6], coefc[:, 0:1], ALU.mult, ALU.add).then_inc(coef_ok, 1)
            layernorm(0, 1, lambda t: dve.wait_ge(ld_x[1], 16))
            for hf in range(2):
                for n in range(4 * hf, 4 * hf + 4):
                    w, blk = (n % 4) // 2, n % 2
                    dve.wait_ge(qk_f, n + 1)
                    dve.wait_ge(qk_h, n + 1)
                    if n >= 2:
                        dve.wait_ge(qk_l, n - 1)
                        dve.wait_ge(qk_m, n - 1)
                    dve.tensor_tensor(tq[:, n % 2, :], fq[:, n % 2, :], parts[:, w, 0, blk, hf * HALF:(hf + 1) * HALF],
                                      ALU.subtract).then_inc(qk_t, 1)
                    dve.wait_ge(qk_m, n + 1)
                    dve.tensor_tensor(parts[:, w, 2, blk, hf * HALF:(hf + 1) * HALF], tq[:, n % 2, :], parts[:, w, 1, blk, hf * HALF:(hf + 1) * HALF],
                                      ALU.subtract).then_inc(qk_l, 1)
                for i, bank in enumerate((ps_o, ps_m)):
                    t = hf * TH + 2 * i
                    dve.wait_ge(v_ps, 2 * hf + i + 1)
                    dve.tensor_copy(vall[:, t:t + 2, :, :],
                                    bank[:].rearrange("p (t h d) -> p t h d", t=2, h=H)).then_inc(v_sb, 1)

            def score_max(n, h):
                dve.wait_ge(s_ready, n + 1)
                dve.tensor_reduce(rmax[:, :, h:h + 1], ps_s[h % 2][:].rearrange("p (t s) -> p t s", t=TB),
                                  AXX, ALU.max).then_inc(s_used, 1)

            def minus_max(b):
                dve.wait_ge(rm_T, b + 1)
                if not isinstance(b, int) or b > 0:
                    dve.wait_ge(aug_in, 32 * b)
                dve.tensor_scalar(nmf[:, 0, :], ps_m[0:2 * H, 0:P], -1.0, None, ALU.mult).then_inc(m_used, 1)
                dve.wait_ge(m_used, M_BEFORE(b, 3) + 1)
                mine.done(dve.tensor_copy(nmp[:, 0, :], nmf[:, 0, :]))
                mine.wait()
                mine.done(dve.tensor_tensor(nmf[:, 1, :], nmf[:, 0, :], nmp[:, 0, :], ALU.subtract))
                mine.wait()
                mine.done(dve.tensor_copy(nmp[:, 1, :], nmf[:, 1, :]))
                mine.wait()
                dve.tensor_tensor(nmp[:, 2, :], nmf[:, 1, :], nmp[:, 1, :], ALU.subtract).then_inc(nm_ready, 1)

            def normalise(b, q):
                dve.wait_ge(bc_ready, 4 * b + q + 1)
                mine.done(dve.reciprocal(rcp, ps_m[:, 0:S]))
                mine.wait()
                if q == 0:
                    dve.wait_ge(pr_ready, b + 1)
                dve.tensor_tensor(onm[:, q, :], osb[:, q, :], rcp, ALU.mult).then_inc(on_ready, 1)

            def M_BEFORE(b, k):
                return 0

            dve.sem_inc(pr_ready, 1)
            for h in range(H):
                score_max(h, h)
            dve.wait_ge(rm_T, 1)

            def minus_max_all(b, base):
                dve.wait_ge(rm_T, b + 1)
                if not (isinstance(b, int) and b == 0):
                    dve.wait_ge(aug_in, 32 * b)
                mine.done(dve.tensor_scalar(nmf[:, 0, :], ps_m[0:2 * H, 0:P], -1.0, None, ALU.mult))
                mine.wait()
                mine.done(dve.tensor_copy(nmp[:, 0, :], nmf[:, 0, :]))
                mine.wait()
                mine.done(dve.tensor_tensor(nmf[:, 1, :], nmf[:, 0, :], nmp[:, 0, :], ALU.subtract))
                mine.wait()
                mine.done(dve.tensor_copy(nmp[:, 1, :], nmf[:, 1, :]))
                mine.wait()
                dve.tensor_tensor(nmp[:, 2, :], nmf[:, 1, :], nmp[:, 1, :], ALU.subtract).then_inc(nm_ready, 1)

            minus_max_all(0, 0)

            def batch(b, more, tok):
                h = 0
                for i in range(8):
                    if more:
                        for _ in range(S_IN_SLOT[i]):
                            score_max(16 * b + 16 + h, h)
                            h += 1
                    if i in (3, 5, 7):
                        normalise(b, (i - 3) // 2)
                    if i == 6 and more:
                        minus_max_all(b + 1, None)
                normalise(b, NQ - 1)
                dve.wait_ge(pr_ready, b + 2)
                dve.scalar_tensor_tensor(out=tok, in0=ps_m[:], scalar=1.0 - LAMBDA_INIT, in1=tok,
                                         op0=ALU.mult, op1=ALU.add).then_inc(x1_ok, 1)

            PER = NQ + 4
            n0 = mine.n
            xflat = xs[:, :, :].rearrange("p t d -> p (t d)")
            with dve.Fori(0, B - 1) as b:
                mine.off = b * PER
                batch(b, True, xflat[:, bass.ds(b * (TB * D), TB * D)])
            assert mine.n == n0 + PER
            mine.off, mine.n = None, n0 + (B - 1) * PER
            batch(B - 1, False, xflat[:, (B - 1) * TB * D:B * TB * D])

            for hf in range(2):
                layernorm(1, hf, lambda t: dve.wait_ge(x1_ok, B))
            for hf in range(2):
                for n in range(8 * hf, 8 * hf + 8):
                    dve.wait_ge(xp_sg, n + 1)
                    if n >= 2:
                        dve.wait_ge(xa_ok, n - 1)
                    dve.tensor_tensor(pm[:, n % 2, :], ps_t[(n % 4) // 2][:, (n % 2) * 512:(n % 2 + 1) * 512],
                                      sg[:, n % 2, :], ALU.mult).then_inc(xp_pm, 1)
                for t in range(hf * TH, hf * TH + TH):
                    dve.wait_ge(xy_ps, t + 1)
                    dve.tensor_tensor(xs[:, t, :], ps_s[t % 2][:, 0:D], xs[:, t, :], ALU.add).then_inc(x2_ok, 1)
            for hf in range(2):
                layernorm(2, hf, lambda t: dve.wait_ge(x2_ok, TT))
            dve.wait_ge(lg_ps, 1)
            mine.done(dve.tensor_copy(lg[:], ps_o[:, 0:TT * E].rearrange("p (t e) -> p t e", t=TT)))
            mine.wait()
            for t in range(TT):
                mine.done(dve.max(mx8[:, t, :], lg[:, t, :]))
            mine.wait()
            for t in range(TT):
                mine.done(dve.max_index(ix8[:, t, :], mx8[:, t, :], lg[:, t, :]))
            dve.tensor_tensor(gw[:, 0, :], mx8[:, :, 1], mx8[:, :, 0], ALU.subtract).then_inc(gd_ok, 1)
            mine.wait()
            mine.done(dve.tensor_copy(ixf[:], ix8[:, :, 0:2]))
            mine.wait()
            for r in range(2):
                mine.done(dve.tensor_tensor(oh[:, r, :, :], iota[:].unsqueeze(1).broadcast_to([P, TT, E]),
                                            ixf[:, :, r:r + 1].broadcast_to([P, TT, E]), ALU.is_equal))
            dve.wait_ge(ge_ok, 1)
            mine.done(dve.tensor_scalar(gw[:, 2, :], gw[:, 1, :], 1.0, None, ALU.add))
            mine.wait()
            mine.done(dve.reciprocal(gw[:, 3, :], gw[:, 2, :]))
            mine.wait()
            mine.done(dve.tensor_tensor(gw[:, 0, :], gw[:, 3, :], gw[:, 1, :], ALU.mult))
            mine.wait()
            for r, w in ((0, 3), (1, 0)):
                mine.done(dve.tensor_tensor(oh[:, r, :, :], oh[:, r, :, :],
                                            gw[:, w, :].unsqueeze(2).broadcast_to([P, TT, E]), ALU.mult))
            mine.wait()
            mine.done(dve.tensor_tensor(cw[:], oh[:, 0, :, :], oh[:, 1, :, :], ALU.add))
            mine.wait()
            for n in range(2 * NJ):
                hf, e = n // NJ, JOBS[n % NJ][3]
                for f in range(FB):
                    m = n * FB + f
                    dve.wait_ge(gu_sg, m + 1)
                    if n >= 2:
                        dve.wait_ge(gy_ps, 4 * (n - 1))
                    dve.tensor_tensor(aT[:, (n % 2) * FB + f, :], ps_t[m % 2][:, 512:1024], sg[:, m % 2, :],
                                      ALU.mult).then_inc(ga_ok, 1)
                for t in range(TH):
                    tk = hf * TH + t
                    m = n * TH + t
                    dve.wait_ge(gy_ps, m + 1)
                    if n >= 1:
                        dve.wait_ge(gy_ok, m - 3)
                    y = ps_s[m % 2][:, 0:D]
                    if e is None:
                        dve.tensor_tensor(xs[:, tk, :], y, xs[:, tk, :], ALU.add).then_inc(gy_ok, 1)
                    else:
                        dve.scalar_tensor_tensor(out=xs[:, tk, :], in0=y, scalar=cw[:, tk, e:e + 1], in1=xs[:, tk, :],
                                                 op0=ALU.mult, op1=ALU.add).then_inc(gy_ok, 1)

        @block.tensor
        def _(pe):
            def transposes(stage, hf, banks):
                for k in range(KD):
                    pe.wait_ge(h_ready, 8 * stage + TH * (hf + 1))
                    n = 4 * stage + 2 * hf + k
                    if n >= 2:
                        pe.wait_ge(hT_sb, n - 1)
                    for t in range(TH):
                        last = pe.transpose(banks[k][:, t * P:(t + 1) * P], hn[:, hf * TH + t, k * P:(k + 1) * P], ident[:])
                    last.then_inc(hT_ps, 1)

            pe.sem_inc(pv_done, 2)
            pe.wait_ge(ld_wqk, 32)
            for hf in range(2):
                tok = slice(hf * HALF, (hf + 1) * HALF)
                transposes(0, hf, ps_s)
                pe.wait_ge(hT_sb, 2 * hf + 2)
                for n in range(4 * hf, 4 * hf + 4):
                    if hf == 1:
                        pe.wait_ge(qk_h, n - 3)
                    bank = ps_t[(n % 4) // 2][:, (n % 2) * 512:(n % 2 + 1) * 512]
                    for k in range(KD):
                        last = pe.matmul(bank, wqk[:, k, (n % 4) * P:(n % 4 + 1) * P], hT[:, k, tok],
                                         start=(k == 0), stop=(k == KD - 1))
                    last.then_inc(qk_ps, 1)
                if hf == 0:
                    pe.wait_ge(ld_wv, 16)
                for i, bank in enumerate((ps_o, ps_m)):
                    if hf == 1:
                        pe.wait_ge(v_sb, i + 1)
                    for t in range(2):
                        tt = hf * TH + 2 * i + t
                        for k in range(KD):
                            last = pe.matmul(bank[:, t * D:(t + 1) * D], hT[:, k, tt * P:(tt + 1) * P], wv[:, k, :],
                                             start=(k == 0), stop=(k == KD - 1))
                    last.then_inc(v_ps, 1)

            def scores(n, h, rows, keys):
                pe.wait_ge(s_used, n + 1)
                for tt in range(TB):
                    last = pe.matmul(ps_s[h % 2][:, tt * S:(tt + 1) * S], rows(h, tt), keys(h), start=True, stop=True)
                last.then_inc(s_ready, 1)

            def rows_of(b):
                return (lambda h, tt: qst[0:KS_ROWS, h, bass.ds(b * S + tt * P, P)],
                        lambda h: kst[0:KS_ROWS, h, bass.ds(b * S, S)])

            def max_rows(b):
                pe.wait_ge(s_used, 16 * b + 18)
                pe.transpose(ps_m[0:2 * H, 0:P], rmax[:, :, :].rearrange("p t h -> p (t h)"), ident[:]).then_inc(rm_T, 1)

            def batch(b, more):
                def exps_in(i):
                    q, st = i // 2, i % 2
                    pe.wait_ge(p_ready, 8 * b + i + 1)
                    for j in range(Q4):
                        h = Q4 * q + j
                        last = pe.matmul(ps_t[i % 2][:, j * S:(j + 1) * S], kst[0:KA_ROWS, h, bass.ds(b * S + st * P, P)],
                                         qst[0:KA_ROWS, h, bass.ds(b * S, S)], start=True, stop=True)
                    last.then_inc(t_ready, 1)

                def values(i):
                    q, st = i // 2, i % 2
                    pe.wait_ge(p_ready, 8 * b + i + 3)
                    if st == 0:
                        pe.wait_ge(o_evac, 4 * b + q + 1)
                    for j in range(Q4):
                        h = Q4 * q + j
                        last = pe.matmul(ps_o[HP * j:HP * (j + 1), 0:S], vaug[:, st, h, :], pt[:, i % 2, j * S:(j + 1) * S],
                                         start=(st == 0), stop=(st == TB - 1))
                    last.then_inc(pv_done, 1)

                def sums(q):
                    pe.wait_ge(o_evac, 4 * b + q + 2)
                    if q > 0:
                        pe.wait_ge(on_ready, 4 * b + q + 4)
                    if q == 2 and more:
                        pe.wait_ge(nm_ready, b + 2)
                    pe.matmul(ps_m[:, 0:S], sel[:], osb[:, q, :], start=True, stop=True).then_inc(bc_ready, 1)

                pe.wait_ge(aug_in, 32 * b + 32)
                pe.wait_ge(vaug_ok, b + 1)
                exps_in(0)
                h = 0
                for i in range(8):
                    if i < 7:
                        exps_in(i + 1)
                    if more:
                        rows, keys = rows_of(b + 1)
                        for _ in range(S_IN_SLOT[i]):
                            scores(16 * b + 16 + h, h, rows, keys)
                            h += 1
                    values(i)
                    if i in (3, 5, 7):
                        sums((i - 3) // 2)
                    if i == 6 and more:
                        pe.wait_ge(on_ready, 4 * b + 6)
                        max_rows(b + 1)
                sums(NQ - 1)
                pe.wait_ge(on_ready, 4 * b + 8)
                for tt in range(TB):
                    for q in range(NQ):
                        last = pe.matmul(ps_m[:, tt * D:(tt + 1) * D], onm[:, q, tt * P:(tt + 1) * P], wp[:, q, :],
                                         start=(q == 0), stop=(q == NQ - 1))
                last.then_inc(pr_ready, 1)
                pe.wait_ge(x1_ok, b + 1)

            pe.wait_ge(qk_in[0], 192)
            rows, keys = rows_of(0)
            for h in range(H):
                scores(h, h, lambda h, tt: qst[0:KS_ROWS, h, tt * P:(tt + 1) * P], lambda h: kst[0:KS_ROWS, h, 0:S])
            pe.wait_ge(v_sb, 4)
            max_rows(0)
            pe.wait_ge(qk_in[1], 192)
            pe.wait_ge(qk_h, 8)
            pe.wait_ge(s_const, 2)
            pe.wait_ge(ld_wp, 16)
            pe.wait_ge(ld_c, 64)
            pe.wait_ge(nm_ready, 1)
            with pe.Fori(0, B - 1) as b:
                batch(b, True)
            batch(B - 1, False)

            for hf in range(2):
                transposes(1, hf, (ps_o, ps_m))
            pe.wait_ge(ld_ct, 16)
            pe.wait_ge(p_ready, 8 * B + 2)
            for hf in range(2):
                tok = slice(hf * HALF, (hf + 1) * HALF)
                pe.wait_ge(hT_sb, 4 + 2 * hf + 2)
                for n in range(8 * hf, 8 * hf + 8):
                    e, fb = (n % 8) // 2, n % 2
                    if n >= 4:
                        pe.wait_ge(xp_pm, n - 3)
                    bank = ps_t[(n % 4) // 2][:, (n % 2) * 512:(n % 2 + 1) * 512]
                    for k in range(KD):
                        last = pe.matmul(bank, ct[:, e, k, fb * P:(fb + 1) * P], hT[:, k, tok],
                                         start=(k == 0), stop=(k == KD - 1))
                    last.then_inc(xp_ps, 1)
                for t in range(TH):
                    tt = hf * TH + t
                    pe.wait_ge(xa_ok, 8 * hf + 8)
                    if tt >= 2:
                        pe.wait_ge(x2_ok, tt - 1)
                    for i in range(8):
                        last = pe.matmul(ps_s[tt % 2][:, 0:D], aT[:, i, t * P:(t + 1) * P], ct[:, i // 2, i % 2, :],
                                         start=(i == 0), stop=(i == 7))
                    last.then_inc(xy_ps, 1)
            for hf in range(2):
                transposes(2, hf, (ps_o, ps_m))
            pe.wait_ge(ld_rw, 16)
            pe.wait_ge(hT_sb, 12)
            for tt in range(TT):
                for k in range(KD):
                    last = pe.matmul(ps_o[:, tt * E:(tt + 1) * E], hT[:, k, tt * P:(tt + 1) * P], rw[:, k, :],
                                     start=(k == 0), stop=(k == KD - 1))
            last.then_inc(lg_ps, 1)
            pe.wait_ge(xp_pm, 16)
            for n in range(2 * NJ):
                hf, s = n // NJ, n % 2
                tok = slice(hf * HALF, (hf + 1) * HALF)
                pe.wait_ge(ld_e[s], 48 * (n // 2 + 1))
                for f in range(FB):
                    m = n * FB + f
                    if m >= 2:
                        pe.wait_ge(ga_ok, m - 1)
                    for o in range(2):
                        for k in range(KD):
                            last = pe.matmul(ps_t[m % 2][:, o * 512:(o + 1) * 512],
                                             wgu[:, 2 * s + o, k, f * P:(f + 1) * P], hT[:, k, tok],
                                             start=(k == 0), stop=(k == KD - 1))
                    last.then_inc(gu_ps, 1)
                pe.wait_ge(ga_ok, FB * (n + 1))
                for t in range(TH):
                    m = n * TH + t
                    if m >= 2:
                        pe.wait_ge(gy_ok, m - 1)
                    else:
                        pe.wait_ge(x2_ok, TT)
                    for f in range(FB):
                        last = pe.matmul(ps_s[m % 2][:, 0:D], aT[:, s * FB + f, t * P:(t + 1) * P], wdn[:, s, f, :],
                                         start=(f == 0), stop=(f == FB - 1))
                    last.then_inc(gy_ps, 1)


def _consts():
    p = np.arange(P)
    ident = np.eye(P, dtype=np.float32)
    sel = (p[:, None] == (p[None, :] // HP) * HP + HD).astype(np.float32)
    first = (p % HD) < HD // 2
    coef = np.stack([np.where(first, SCALE, 0.0), np.where(first, 0.0, -SCALE)], axis=1).astype(np.float32)
    iota = np.tile(np.arange(E, dtype=np.float32), (P, 1))
    return {"ident": ident, "sel": sel, "coef": coef, "iota": iota}


def kernel(x, itok_BxS_13_99985, ctx_2048, L0_attn_W_attn, L0_attn_W_proj, L0_attn_lambda_q1, L0_attn_lambda_k1,
           L0_attn_lambda_q2, L0_attn_lambda_k2, L0_ffn_router_w, L0_ffn_w1, L0_ffn_w2, L0_ffn_w_gate, L0_ffn_w_up,
           L0_ffn_w_down):
    import concourse.bacc as _bacc
    from concourse.bass_utils import run_bass_kernel_spmd as _run

    C = D // 2
    w = np.asarray(L0_attn_W_attn)
    q1, k1, q2, k2 = (w[:, i * C:(i + 1) * C].reshape(D, H, HD // 2) for i in range(4))
    wq = np.concatenate([q1, q2], axis=2).reshape(D, D)
    wk = np.concatenate([k1, k2], axis=2).reshape(D, D)
    wqk = np.concatenate([wq, wk], axis=1).reshape(KD, P, 2 * D).transpose(1, 0, 2)
    wv = w[:, 4 * C:].reshape(KD, P, D).transpose(1, 0, 2)
    wp = np.zeros((NQ, Q4, HP, D), np.float32)
    wp[:, :, :HD, :] = np.asarray(L0_attn_W_proj).reshape(NQ, Q4, HD, D)
    wp = wp.reshape(NQ, P, D).transpose(1, 0, 2)
    ctxT = np.asarray(ctx_2048).transpose(2, 0, 1).reshape(KD, P, XE, D).transpose(1, 2, 0, 3)
    lam_vecs = np.stack([np.asarray(L0_attn_lambda_q1), np.asarray(L0_attn_lambda_k1),
                         np.asarray(L0_attn_lambda_q2), np.asarray(L0_attn_lambda_k2)])
    c = _consts()
    arrays = {
        "x": x, "ids": np.asarray(itok_BxS_13_99985).reshape(T), "ctxT": ctxT, "w_qk": wqk, "w_v": wv, "w_proj": wp,
        "lam_vecs": lam_vecs, "router_w": L0_ffn_router_w, "w1": L0_ffn_w1, "w2": L0_ffn_w2,
        "w_gate": L0_ffn_w_gate, "w_up": L0_ffn_w_up, "w_down": L0_ffn_w_down,
        "ident_c": c["ident"], "sel_c": c["sel"], "coef_c": c["coef"], "iota_c": c["iota"],
    }
    nc = _bacc.Bacc("TRN2", target_bir_lowering=False, num_devices=1)
    feeds, args = {}, []
    for name, a in arrays.items():
        a = np.ascontiguousarray(a)
        feeds[f"in_{name}"] = a
        args.append(nc.dram_tensor(f"in_{name}", a.shape, mybir.dt.from_np(a.dtype), kind="ExternalInput").ap())
    args.append(nc.dram_tensor("out_0", (B, S, D), F32, kind="ExternalOutput").ap())
    decoder_layer(nc, *args)
    r = _run(nc, [feeds], core_ids=[0])
    return r.results[0]["out_0"]
```

```python
from contextlib import ExitStack

import numpy as np

import concourse.bass as bass
from concourse import mybir

F32 = mybir.dt.float32
BF16 = mybir.dt.bfloat16
I32 = mybir.dt.int32
U32 = mybir.dt.uint32
ALU = mybir.AluOpType
ACT = mybir.ActivationFunctionType
AXX = mybir.AxisListType.X

P = 128
B, S, D = 4, 256, 256
T = B * S
TT = T // P
TB = S // P
HALF = T // 2
TH = HALF // P
KD = D // P
H = 16
HD = D // H
HP = 32
Q4 = 4
NQ = H // Q4
LAMBDA_INIT = 0.2
SCALE = float(HD // 2) ** -0.5
EPS = 1e-5
Q_PARTS = (0, 0, 1, 0, 2, 1)
K_PARTS = (0, 1, 0, 2, 0, 1)
NT = len(Q_PARTS)
KS_ROWS = NT * HD
KA_ROWS = KS_ROWS + 3
XE = 4
VOCAB = 12500
PER_X = VOCAB // XE
E = 8
INTER = 512
SHARED = 1024
NM = (T * 2 + E * (P - 1)) // P
MAGIC = float(0x5F3759DF)

S_IN_SLOT = (3, 3, 3, 3, 3, 1, 0, 0)


def decoder_layer(nc, x, ids, ctxT, w_qk, w_v, w_proj, lam_vecs, router_w, w1, w2, w_gate, w_up, w_down,
                  ident_c, sel_c, coef_c, iota_c, before_c, tiles_c, out):
    with ExitStack() as ctx:
        def sb(name, shape, dt=F32):
            return ctx.enter_context(nc.sbuf_tensor(name, shape, dt))

        def sem(name):
            return ctx.enter_context(nc.semaphore(name))

        xs = sb("xs", [P, TT, D])
        hn = sb("hn", [P, TT, D])
        hT = sb("hT", [P, KD, T])
        st6 = sb("st6", [P, TT, 6])
        mv = sb("mv", [P, TT, 2])
        nw = sb("nw", [P, 6, TT])
        pre = sb("pre", [P, 6144])
        wqk = pre[:, 0:1024].rearrange("p (k n) -> p k n", k=KD)
        wv = pre[:, 1024:1536].rearrange("p (k n) -> p k n", k=KD)
        wp = pre[:, 1536:2560].rearrange("p (q n) -> p q n", q=NQ)
        fq = pre[:, 2560:3584].rearrange("p (s t) -> p s t", s=2)
        tq = pre[:, 3584:4608].rearrange("p (s t) -> p s t", s=2)
        idf = pre[:, 4608:5632]
        wsg = pre[:, 0:4096].rearrange("p (o k f) -> p o k f", o=2, k=KD)
        wsd = pre[:, 4096:6144].rearrange("p (k n) -> p k n", k=SHARED // P)
        ident = sb("ident", [P, P])
        sel = sb("sel", [P, P])
        coefc = sb("coefc", [P, 2])
        lamv = sb("lamv", [P, 4, D])
        lam = sb("lam", [P, 8])
        coef = sb("coef", [P, 1])
        big = sb("big", [P, 24576])
        qst = big[:, 0:8192].bitcast(BF16).rearrange("p (h t) -> p h t", h=H)
        kst = big[:, 8192:16384].bitcast(BF16).rearrange("p (h t) -> p h t", h=H)
        vall = big[:, 16384:18432].rearrange("p (t h d) -> p t h d", t=TT, h=H)
        vaug = big[:, 18432:19456].rearrange("p (t h d) -> p t h d", t=TB, h=H)
        pt = big[:, 19456:21504].rearrange("p (s n) -> p s n", s=2)
        osb = big[:, 21504:22528].rearrange("p (q t) -> p q t", q=NQ)
        onm = big[:, 22528:23552].rearrange("p (q t) -> p q t", q=NQ)
        rcp = big[:, 23552:23808]
        mid = sb("mid", [P, 6144])
        parts = mid[:, :].bitcast(BF16).rearrange("p (w j b t) -> p w j b t", w=2, j=3, b=2)
        rmax = sb("rmax", [P, TB, H])
        nmf = sb("nmf", [2 * H, 2, P])
        nmp = sb("nmp", [2 * H, 3, P], BF16)
        ct = sb("ct", [P, XE, KD, D])
        moe = sb("moe", [P, 3584])
        xmask = moe[:, 0:2048].bitcast(BF16).rearrange("p (e t) -> p e t", e=XE)
        xt = moe[:, 0:512].rearrange("p (s d) -> p s d", s=2)
        xtT = moe[:, 512:1024].rearrange("p (s t) -> p s t", s=2)
        ma = moe[:, 1024:2048].rearrange("p (s f) -> p s f", s=2)
        maT = moe[:, 2048:3072].rearrange("p (s f) -> p s f", s=2)
        ysb = moe[:, 3072:3584].rearrange("p (s d) -> p s d", s=2)
        idb = moe[:, 2048:3072].bitcast(I32)
        zrow = sb("zrow", [P, D])
        before = sb("before", [P, P])
        beforeb = sb("beforeb", [P, P], BF16)
        onesb = sb("onesb", [P, P], BF16)
        tiles = sb("tiles", [1, NM, E - 1])
        tge = sb("tge", [1, NM, E - 1])
        eidf = sb("eidf", [1, NM])
        eid = sb("eid", [1, NM], I32)
        chosen = sb("chosen", [P, TT, E], BF16)
        cnt = sb("cnt", [P, 6, E])
        posf = sb("posf", [P, TT, E])
        posm = sb("posm", [P, 2, TT, E])
        posr = sb("posr", [P, 2, TT])
        pos = sb("pos", [P, 2 * TT], U32)
        xge = sb("xge", [P, 2, T], BF16)
        aT = mid[:, 0:4096].rearrange("p (f t) -> p f t", f=8)
        sg = mid[:, 4096:5120].rearrange("p (s t) -> p s t", s=2)
        pm = mid[:, 5120:6144].rearrange("p (s t) -> p s t", s=2)
        msg = pm
        rw = sb("rw", [P, KD, E])
        iota = sb("iota", [P, E])
        lg = sb("lg", [P, TT, E])
        mx8 = sb("mx8", [P, TT, 8])
        ix8 = sb("ix8", [P, TT, 8], U32)
        ixf = sb("ixf", [P, TT, 2])
        oh = sb("oh", [P, 2, TT, E])
        gw = sb("gw", [P, 4, TT])
        W1S, W2S, W2O = KD * 2 * INTER, INTER // P * D, E * KD * 2 * INTER
        w1v = big[:, 0:W2O].rearrange("p (e k f) -> p e k f", e=E, k=KD)
        w2v = big[:, W2O:W2O + E * W2S].rearrange("p (e k n) -> p e k n", e=E, k=INTER // P)
        gat = big[:, 0:2 * TT * D].rearrange("p (r t d) -> p r t d", r=2, t=TT)

        ps_s = [ctx.enter_context(nc.psum_tensor(f"ps_s{i}", [P, 512], F32)) for i in range(2)]
        ps_t = [ctx.enter_context(nc.psum_tensor(f"ps_t{i}", [P, 1024], F32)) for i in range(2)]
        ps_o = ctx.enter_context(nc.psum_tensor("ps_o", [P, 512], F32))
        ps_m = ctx.enter_context(nc.psum_tensor("ps_m", [P, 512], F32))

        qk_dram = nc.dram_tensor("qk_parts", (2, 3, KD, P, T), BF16, kind="Internal").ap()
        xp_dram = nc.dram_tensor("routed_rows", (NM * P, D), F32, kind="Internal").ap()
        yp_dram = nc.dram_tensor("routed_out", (NM * P, D), F32, kind="Internal").ap()
        mx_dram = nc.dram_tensor("mx_parts", (3, TB, H, P), BF16, kind="Internal").ap()

        ld_x = [sem(f"ld_x{i}") for i in range(2)]
        ld_c = sem("ld_c")
        ld_ids = sem("ld_ids")
        ld_wqk = sem("ld_wqk")
        ld_wv = sem("ld_wv")
        ld_wp = sem("ld_wp")
        ld_ct = sem("ld_ct")
        ld_rw = sem("ld_rw")
        s_const = sem("s_const")
        dve_step = sem("dve_step")
        act_step = sem("act_step")
        coef_ok = sem("coef_ok")
        lam_dot = sem("lam_dot")
        lam_exp = sem("lam_exp")
        h_ready = sem("h_ready")
        hT_ps = sem("hT_ps")
        hT_sb = sem("hT_sb")
        qk_ps = sem("qk_ps")
        qk_f = sem("qk_f")
        qk_h = sem("qk_h")
        qk_t = sem("qk_t")
        qk_m = sem("qk_m")
        qk_l = sem("qk_l")
        qk_out = [sem(f"qk_out{i}") for i in range(2)]
        qk_in = [sem(f"qk_in{i}") for i in range(2)]
        v_ps = sem("v_ps")
        v_sb = sem("v_sb")
        s_ready = sem("s_ready")
        s_used = sem("s_used")
        rm_T = sem("rm_T")
        nm_ready = sem("nm_ready")
        aug_out = sem("aug_out")
        aug_in = sem("aug_in")
        t_ready = sem("t_ready")
        p_ready = sem("p_ready")
        pv_done = sem("pv_done")
        o_evac = sem("o_evac")
        bc_ready = sem("bc_ready")
        m_used = sem("m_used")
        on_ready = sem("on_ready")
        pr_ready = sem("pr_ready")
        vaug_ok = sem("vaug_ok")
        x1_ok = sem("x1_ok")
        mask_ok = sem("mask_ok")
        pool_step = sem("pool_step")
        xp_ps = sem("xp_ps")
        xp_sg = sem("xp_sg")
        xp_pm = sem("xp_pm")
        xa_ok = sem("xa_ok")
        xy_ps = sem("xy_ps")
        x2_ok = sem("x2_ok")
        lg_ps = sem("lg_ps")
        lg_sb = sem("lg_sb")
        gd_ok = sem("gd_ok")
        ge_ok = sem("ge_ok")
        ch_ok = sem("ch_ok")
        rk_ps = sem("rk_ps")
        pos_ok = sem("pos_ok")
        eid_ok = sem("eid_ok")
        lt_ok = sem("lt_ok")
        ld_lt = sem("ld_lt")
        ld_ws = sem("ld_ws")
        ld_we = sem("ld_we")
        zr_ok = sem("zr_ok")
        zr_out = sem("zr_out")
        scat = sem("scat")
        gu_ps = sem("gu_ps")
        gu_sg = sem("gu_sg")
        ga_ok = sem("ga_ok")
        gy_ps = sem("gy_ps")
        gy_ok = sem("gy_ok")
        xT_ps = sem("xT_ps")
        xT_sb = sem("xT_sb")
        mg_ps = sem("mg_ps")
        mu_ps = sem("mu_ps")
        m_sg = sem("m_sg")
        ma_ok = sem("ma_ok")
        at_ps = sem("at_ps")
        at_sb = sem("at_sb")
        my_ps = sem("my_ps")
        my_sb = sem("my_sb")
        y_out = [sem(f"y_out{i}") for i in range(2)]
        s_out = sem("s_out")
        fin_ok = sem("fin_ok")
        ld_xt = [sem(f"ld_xt{i}") for i in range(2)]
        gath = [sem(f"gath{i}") for i in range(2)]

        x_rows = x.rearrange("b (s p) d -> p (b s) d", p=P)
        out_rows = out.rearrange("b (s p) d -> p (b s) d", p=P)

        FS, FB = SHARED // P, INTER // P

        block = ctx.enter_context(nc.Block())

        class Steps:

            def __init__(self, eng, s):
                self.eng, self.s, self.n, self.off = eng, s, 0, None

            def done(self, ins):
                self.n += 1
                ins.then_inc(self.s, 1)

            def wait(self):
                self.eng.wait_ge(self.s, self.n if self.off is None else self.off + self.n)

        @block.sync
        def _(sp):
            for hf in range(2):
                sp.dma_start(xs[:, hf * TH:(hf + 1) * TH, :], x_rows[:, hf * TH:(hf + 1) * TH, :]).then_inc(ld_x[hf], 16)
            sp.dma_start(lamv[:], lam_vecs.partition_broadcast(P)).then_inc(ld_c, 16)
            sp.dma_start(coefc[:], coef_c).then_inc(ld_c, 16)
            sp.dma_start(iota[:], iota_c).then_inc(ld_c, 16)
            sp.dma_start(before[:], before_c).then_inc(ld_lt, 16)
            sp.dma_start(tiles[:], tiles_c).then_inc(ld_lt, 16)
            sp.dma_start(sel[:], sel_c).then_inc(ld_c, 16)
            sp.dma_start(wp[:], w_proj).then_inc(ld_wp, 16)
            sp.dma_start(idb, ids.partition_broadcast(P)).then_inc(ld_ids, 16)
            sp.dma_start(rw[:], router_w.rearrange("(k p) e -> p k e", p=P)).then_inc(ld_rw, 16)
            for hf in range(2):
                tok = slice(hf * HALF, (hf + 1) * HALF)
                for w in range(2):
                    sp.wait_ge(qk_h, 4 * hf + 2 * w + 2)
                    sp.wait_ge(qk_m, 4 * hf + 2 * w + 2)
                    sp.wait_ge(qk_l, 4 * hf + 2 * w + 2)
                    for j in range(3):
                        sp.dma_start(qk_dram[w, j, :, :, tok].rearrange("b p t -> p b t"),
                                     parts[:, w, j, :, tok]).then_inc(qk_out[hf], 16)
                sp.wait_ge(qk_out[hf], 96)
                for dst, w, of in ((qst, 0, Q_PARTS), (kst, 1, K_PARTS)):
                    for j, part in enumerate(of):
                        src = qk_dram[w, part, :, :, tok].rearrange("b (h d) t -> d (b h) t", d=HD)
                        sp.dma_start(dst[HD * j:HD * (j + 1), :, tok], src).then_inc(qk_in[hf], 16)
                if hf == 0:
                    sp.dma_start(ct[:], ctxT).then_inc(ld_ct, 16)
            sp.wait_ge(zr_ok, 1)
            sp.dma_start(xp_dram.rearrange("(n p) d -> p n d", p=P),
                         zrow[:].unsqueeze(1).broadcast_to([P, NM, D])).then_inc(zr_out, 16)

            def aug(b):
                sp.wait_ge(nm_ready, b + 1)
                sp.dma_start(mx_dram.rearrange("j t h n -> (t h) j n"), nmp[:, :, :]).then_inc(aug_out, 16)
                sp.wait_ge(aug_out, 16 * b + 16)
                for tt in range(TB):
                    sp.dma_start(qst[KS_ROWS:KA_ROWS, :, bass.ds(b * S + tt * P, P)],
                                 mx_dram[:, tt, :, :]).then_inc(aug_in, 16)

            aug(0)
            with sp.Fori(1, B) as b:
                aug(b)
            sp.wait_ge(pr_ready, B + 1)
            sp.wait_ge(mask_ok, 1)
            for o, w in enumerate((w_gate, w_up)):
                sp.dma_start(wsg[:, o, :, :], w.rearrange("(k p) f -> p k f", p=P)).then_inc(ld_ws, 16)
            sp.dma_start(wsd, w_down.rearrange("(k p) n -> p k n", p=P)).then_inc(ld_ws, 16)
            for e in range(E):
                sp.dma_start(w1v[:, e, :, :], w1[e].rearrange("(k p) f -> p k f", p=P)).then_inc(ld_we, 16)
                sp.dma_start(w2v[:, e, :, :], w2[e].rearrange("(k p) n -> p k n", p=P)).then_inc(ld_we, 16)

            def load_rows(i, par):
                sp.wait_ge(xT_ps, i + 1)
                sp.dma_start(xt[:, par, :], xp_dram[bass.ds(i * P, P), :]).then_inc(ld_xt[par], 16)

            sp.wait_ge(scat, 16 * 2 * TT)
            with sp.Fori(0, NM // 2) as j:
                for par in range(2):
                    load_rows(2 * j + par, par)
            load_rows(NM - 1, 0)
            for hf in range(2):
                sp.wait_ge(fin_ok, TH * (hf + 1))
                sp.dma_start(out_rows[:, hf * TH:(hf + 1) * TH, :], xs[:, hf * TH:(hf + 1) * TH, :]).then_inc(s_out, 16)
            sp.wait_ge(s_out, 32)

        @block.gpsimd
        def _(pool):
            pool.memset(vaug[:, :, :, :], 0.0).then_inc(pool_step, 1)
            pool.wait_ge(pool_step, 1)
            pool.memset(vaug[:, :, :, HD:HD + 1], 1.0).then_inc(s_const, 1)
            pool.wait_ge(s_const, 1)
            pool.memset(kst[KS_ROWS:KA_ROWS, :, :], 1.0).then_inc(s_const, 1)
            pool.wait_ge(s_const, 2)
            pool.memset(zrow[:], 0.0).then_inc(zr_ok, 1)
            pool.memset(onesb[:], 1.0).then_inc(lt_ok, 1)
            pool.wait_ge(ld_lt, 32)
            pool.tensor_copy(beforeb[:], before[:]).then_inc(lt_ok, 1)
            steps = 1
            for hf in range(2):
                for n in range(4 * hf, 4 * hf + 4):
                    w, blk = (n % 4) // 2, n % 2
                    pool.wait_ge(qk_t, n + 1)
                    pool.tensor_copy(parts[:, w, 1, blk, hf * HALF:(hf + 1) * HALF], tq[:, n % 2, :]).then_inc(qk_m, 1)
            pool.wait_ge(ld_ids, 16)
            pool.tensor_copy(idf, idb).then_inc(pool_step, 1)
            steps += 1
            pool.wait_ge(pool_step, steps)
            for e in range(1, XE):
                a, c = (e - 1) % 2, e % 2
                if e == 1:
                    pool.memset(xge[:, 0, :], 1.0).then_inc(pool_step, 1)
                    steps += 1
                pool.tensor_scalar(xge[:, c, :], idf, float(PER_X * e), None, ALU.is_ge).then_inc(pool_step, 1)
                steps += 1
                pool.wait_ge(pool_step, steps)
                pool.tensor_tensor(xmask[:, e - 1, :], xge[:, a, :], xge[:, c, :], ALU.subtract).then_inc(pool_step, 1)
                steps += 1
                pool.wait_ge(pool_step, steps)
                if e == XE - 1:
                    pool.tensor_copy(xmask[:, e, :], xge[:, c, :]).then_inc(mask_ok, 1)

            def vcopy(b, src):
                pool.wait_ge(pv_done, 8 * b + 2)
                pool.tensor_copy(vaug[:, :, :, 0:HD], src).then_inc(vaug_ok, 1)

            pool.wait_ge(v_sb, 4)
            pool.wait_ge(s_const, 2)
            with pool.Fori(0, B) as b:
                vcopy(b, vall[:, bass.ds(b * TB, TB), :, :])
            pool.wait_ge(mask_ok, 1)
            for n in range(2 * XE * KD):
                hf, e, fb = n // 8, (n % 8) // 2, n % 2
                pool.wait_ge(xp_pm, n + 1)
                if hf == 1:
                    pool.wait_ge(xy_ps, TH)
                pool.tensor_tensor(aT[:, n % 8, :], pm[:, n % 2, :], xmask[:, e, hf * HALF:(hf + 1) * HALF],
                                   ALU.mult).then_inc(xa_ok, 1)
            pool.wait_ge(pos_ok, 1)
            pool.wait_ge(zr_out, 16)
            for t in range(TT):
                for r in range(2):
                    pool.indirect_dma_start(out=xp_dram[:, :],
                                            out_offset=bass.IndirectOffsetOnAxis(ap=pos[:, r * TT + t:r * TT + t + 1], axis=0),
                                            in_=hn[:, t, :], in_offset=None).then_inc(scat, 16)

            def store_rows(i, par):
                pool.wait_ge(my_sb, i + 3)
                pool.dma_start(yp_dram[bass.ds(i * P, P), :], ysb[:, par, :]).then_inc(y_out[par], 16)

            with pool.Fori(0, NM // 2) as j:
                for par in range(2):
                    store_rows(2 * j + par, par)
            store_rows(NM - 1, 0)
            pool.wait_ge(y_out[0], 16 * (NM // 2 + 1))
            pool.wait_ge(y_out[1], 16 * (NM // 2))
            for t in range(TT):
                for r in range(2):
                    pool.indirect_dma_start(out=gat[:, r, t, :], out_offset=None, in_=yp_dram[:, :],
                                            in_offset=bass.IndirectOffsetOnAxis(ap=pos[:, r * TT + t:r * TT + t + 1], axis=0),
                                            ).then_inc(gath[t // TH], 16)

        @block.scalar
        def _(act):
            act.dma_start(ident[:], ident_c).then_inc(ld_wqk, 16)
            act.dma_start(wqk[:], w_qk).then_inc(ld_wqk, 16)
            act.dma_start(wv[:], w_v).then_inc(ld_wv, 16)
            act.sem_inc(p_ready, 2)
            act.sem_inc(o_evac, 1)
            act.wait_ge(lam_dot, 2)
            act.activation(lam[:, 2:4], lam[:, 0:2], ACT.Exp).then_inc(lam_exp, 1)

            def evac_hT(stage, hf, banks):
                for k in range(KD):
                    n = 4 * stage + 2 * hf + k + 1
                    act.wait_ge(hT_ps, n)
                    act.activation(hT[:, k, hf * HALF:(hf + 1) * HALF], banks[k], ACT.Copy).then_inc(hT_sb, 1)

            for hf in range(2):
                evac_hT(0, hf, (ps_s[0][:], ps_s[1][:]))
                if hf == 0:
                    act.wait_ge(coef_ok, 1)
                for n in range(4 * hf, 4 * hf + 4):
                    w, blk = (n % 4) // 2, n % 2
                    bank = ps_t[(n % 4) // 2][:, (n % 2) * 512:(n % 2 + 1) * 512]
                    act.wait_ge(qk_ps, n + 1)
                    if n >= 2:
                        act.wait_ge(qk_t, n - 1)
                    sc = coef[:, 0:1] if w == 0 else 1.0
                    act.activation(fq[:, n % 2, :], bank, ACT.Copy, scale=sc).then_inc(qk_f, 1)
                    act.activation(parts[:, w, 0, blk, hf * HALF:(hf + 1) * HALF], bank, ACT.Copy, scale=sc).then_inc(qk_h, 1)

            def batch(b):
                for i in range(8):
                    act.wait_ge(t_ready, 8 * b + i + 1)
                    act.wait_ge(pv_done, 8 * b + i + 1)
                    act.activation(pt[:, i % 2, :], ps_t[i % 2][:], ACT.Exp).then_inc(p_ready, 1)
                    if (i % 2 == 0 and i > 0) or i == 7:
                        q = i // 2 - 1 if i < 7 else NQ - 1
                        act.wait_ge(pv_done, 8 * b + 2 * q + 4)
                        act.wait_ge(on_ready, 4 * b + q + 1)
                        act.activation(osb[:, q, :], ps_o[:, 0:S], ACT.Copy).then_inc(o_evac, 1)

            with act.Fori(0, B) as b:
                batch(b)

            LB = (ps_o[:], ps_m[:])
            for hf in range(2):
                evac_hT(1, hf, LB)
            for n in range(2 * XE * KD):
                act.wait_ge(xp_ps, n + 1)
                if n >= 2:
                    act.wait_ge(xp_pm, n - 1)
                act.activation(sg[:, n % 2, :], ps_t[(n % 4) // 2][:, (n % 2) * 512:(n % 2 + 1) * 512],
                               ACT.Silu).then_inc(xp_sg, 1)
            for hf in range(2):
                evac_hT(2, hf, LB)
            act.wait_ge(gd_ok, 1)
            act.activation(gw[:, 1, :], gw[:, 0, :], ACT.Exp).then_inc(ge_ok, 1)

            def shared_act(hf):
                for f in range(FS):
                    m = FS * hf + f
                    act.wait_ge(gu_ps, m + 1)
                    if m >= 2:
                        act.wait_ge(ga_ok, m - 1)
                    act.activation(sg[:, m % 2, :], ps_t[m % 2][:, 0:512], ACT.Silu).then_inc(gu_sg, 1)

            def tile_in(i, par):
                act.wait_ge(xT_ps, i + 3)
                act.wait_ge(mu_ps, i + 1)
                act.activation(xtT[:, par, :], ps_o[:, 0:D], ACT.Copy).then_inc(xT_sb, 1)

            def tile_silu(i, par):
                act.wait_ge(mg_ps, i + 1)
                act.wait_ge(ma_ok, i + 1)
                act.activation(msg[:, par, :], ps_t[par][:, 0:INTER], ACT.Silu).then_inc(m_sg, 1)

            def tile_turn(i, par):
                act.wait_ge(at_ps, i + 3)
                act.wait_ge(my_ps, i + 1)
                act.activation(maT[:, par, :], ps_m[:], ACT.Copy).then_inc(at_sb, 1)

            shared_act(0)
            tile_in(0, 0)
            tile_silu(0, 0)
            with act.Fori(0, NM // 2) as j:
                for par in range(2):
                    i = 2 * j + par
                    tile_in(i + 1, 1 - par)
                    tile_turn(i, par)
                    tile_silu(i + 1, 1 - par)
            tile_turn(NM - 1, 0)
            shared_act(1)

        @block.vector
        def _(dve):
            mine = Steps(dve, dve_step)
            dve.sem_inc(s_used, 2)
            dve.sem_inc(on_ready, NQ)

            def layernorm(stage, hf, arrived):
                t0 = hf * TH
                for t in range(t0, t0 + TH):
                    arrived(t)
                    mine.done(dve.bn_stats(st6[:, t, :], xs[:, t, :]))
                mine.wait()
                for t in range(t0, t0 + TH):
                    mine.done(dve.bn_aggr(mv[:, t, :], st6[:, t, :]))
                mine.wait()
                ts = slice(t0, t0 + TH)
                var, half, y, a, c = (nw[:, i, ts] for i in range(5))
                mine.done(dve.tensor_scalar(var, mv[:, ts, 1], EPS, None, ALU.add))
                mine.wait()
                mine.done(dve.tensor_scalar(half.bitcast(I32), var.bitcast(I32), 1, None, ALU.logical_shift_right))
                mine.wait()
                mine.done(dve.tensor_scalar(y.bitcast(I32), half.bitcast(I32), -1.0, MAGIC, ALU.mult, ALU.add))
                mine.wait()
                for _ in range(4):
                    mine.done(dve.tensor_tensor(a, y, y, ALU.mult))
                    mine.wait()
                    mine.done(dve.scalar_tensor_tensor(out=c, in0=a, scalar=-0.5, in1=var, op0=ALU.mult, op1=ALU.mult))
                    mine.wait()
                    mine.done(dve.scalar_tensor_tensor(out=y, in0=c, scalar=1.5, in1=y, op0=ALU.add, op1=ALU.mult))
                    mine.wait()
                for t in range(t0, t0 + TH):
                    dve.tensor_scalar(hn[:, t, :], xs[:, t, :], mv[:, t, 0:1], nw[:, 2, t:t + 1],
                                      ALU.subtract, ALU.mult).then_inc(h_ready, 1)

            layernorm(0, 0, lambda t: dve.wait_ge(ld_x[0], 16))
            dve.wait_ge(ld_c, 64)
            for i in range(2):
                dve.tensor_tensor_reduce(lamv[:, 2 * i, :], lamv[:, 2 * i, :], lamv[:, 2 * i + 1, :], 1.0, 0.0,
                                         ALU.mult, ALU.add, lam[:, i:i + 1]).then_inc(lam_dot, 1)
            dve.wait_ge(lam_exp, 1)
            mine.done(dve.tensor_tensor(lam[:, 4:5], lam[:, 2:3], lam[:, 3:4], ALU.subtract))
            mine.wait()
            mine.done(dve.tensor_scalar(lam[:, 5:6], lam[:, 4:5], LAMBDA_INIT, None, ALU.add))
            mine.wait()
            dve.tensor_scalar(coef[:], coefc[:, 1:2], lam[:, 5:6], coefc[:, 0:1], ALU.mult, ALU.add).then_inc(coef_ok, 1)
            layernorm(0, 1, lambda t: dve.wait_ge(ld_x[1], 16))
            for hf in range(2):
                for n in range(4 * hf, 4 * hf + 4):
                    w, blk = (n % 4) // 2, n % 2
                    dve.wait_ge(qk_f, n + 1)
                    dve.wait_ge(qk_h, n + 1)
                    if n >= 2:
                        dve.wait_ge(qk_l, n - 1)
                        dve.wait_ge(qk_m, n - 1)
                    dve.tensor_tensor(tq[:, n % 2, :], fq[:, n % 2, :], parts[:, w, 0, blk, hf * HALF:(hf + 1) * HALF],
                                      ALU.subtract).then_inc(qk_t, 1)
                    dve.wait_ge(qk_m, n + 1)
                    dve.tensor_tensor(parts[:, w, 2, blk, hf * HALF:(hf + 1) * HALF], tq[:, n % 2, :], parts[:, w, 1, blk, hf * HALF:(hf + 1) * HALF],
                                      ALU.subtract).then_inc(qk_l, 1)
                for i, bank in enumerate((ps_o, ps_m)):
                    t = hf * TH + 2 * i
                    dve.wait_ge(v_ps, 2 * hf + i + 1)
                    dve.tensor_copy(vall[:, t:t + 2, :, :],
                                    bank[:].rearrange("p (t h d) -> p t h d", t=2, h=H)).then_inc(v_sb, 1)

            def score_max(n, h):
                dve.wait_ge(s_ready, n + 1)
                dve.tensor_reduce(rmax[:, :, h:h + 1], ps_s[h % 2][:].rearrange("p (t s) -> p t s", t=TB),
                                  AXX, ALU.max).then_inc(s_used, 1)

            def minus_max(b):
                dve.wait_ge(rm_T, b + 1)
                if not isinstance(b, int) or b > 0:
                    dve.wait_ge(aug_in, 32 * b)
                dve.tensor_scalar(nmf[:, 0, :], ps_m[0:2 * H, 0:P], -1.0, None, ALU.mult).then_inc(m_used, 1)
                dve.wait_ge(m_used, M_BEFORE(b, 3) + 1)
                mine.done(dve.tensor_copy(nmp[:, 0, :], nmf[:, 0, :]))
                mine.wait()
                mine.done(dve.tensor_tensor(nmf[:, 1, :], nmf[:, 0, :], nmp[:, 0, :], ALU.subtract))
                mine.wait()
                mine.done(dve.tensor_copy(nmp[:, 1, :], nmf[:, 1, :]))
                mine.wait()
                dve.tensor_tensor(nmp[:, 2, :], nmf[:, 1, :], nmp[:, 1, :], ALU.subtract).then_inc(nm_ready, 1)

            def normalise(b, q):
                dve.wait_ge(bc_ready, 4 * b + q + 1)
                mine.done(dve.reciprocal(rcp, ps_m[:, 0:S]))
                mine.wait()
                if q == 0:
                    dve.wait_ge(pr_ready, b + 1)
                dve.tensor_tensor(onm[:, q, :], osb[:, q, :], rcp, ALU.mult).then_inc(on_ready, 1)

            def M_BEFORE(b, k):
                return 0

            dve.sem_inc(pr_ready, 1)
            for h in range(H):
                score_max(h, h)
            dve.wait_ge(rm_T, 1)

            def minus_max_all(b, base):
                dve.wait_ge(rm_T, b + 1)
                if not (isinstance(b, int) and b == 0):
                    dve.wait_ge(aug_in, 32 * b)
                mine.done(dve.tensor_scalar(nmf[:, 0, :], ps_m[0:2 * H, 0:P], -1.0, None, ALU.mult))
                mine.wait()
                mine.done(dve.tensor_copy(nmp[:, 0, :], nmf[:, 0, :]))
                mine.wait()
                mine.done(dve.tensor_tensor(nmf[:, 1, :], nmf[:, 0, :], nmp[:, 0, :], ALU.subtract))
                mine.wait()
                mine.done(dve.tensor_copy(nmp[:, 1, :], nmf[:, 1, :]))
                mine.wait()
                dve.tensor_tensor(nmp[:, 2, :], nmf[:, 1, :], nmp[:, 1, :], ALU.subtract).then_inc(nm_ready, 1)

            minus_max_all(0, 0)

            def batch(b, more, tok):
                h = 0
                for i in range(8):
                    if more:
                        for _ in range(S_IN_SLOT[i]):
                            score_max(16 * b + 16 + h, h)
                            h += 1
                    if i in (3, 5, 7):
                        normalise(b, (i - 3) // 2)
                    if i == 6 and more:
                        minus_max_all(b + 1, None)
                normalise(b, NQ - 1)
                dve.wait_ge(pr_ready, b + 2)
                dve.scalar_tensor_tensor(out=tok, in0=ps_m[:], scalar=1.0 - LAMBDA_INIT, in1=tok,
                                         op0=ALU.mult, op1=ALU.add).then_inc(x1_ok, 1)

            PER = NQ + 4
            n0 = mine.n
            xflat = xs[:, :, :].rearrange("p t d -> p (t d)")
            with dve.Fori(0, B - 1) as b:
                mine.off = b * PER
                batch(b, True, xflat[:, bass.ds(b * (TB * D), TB * D)])
            assert mine.n == n0 + PER
            mine.off, mine.n = None, n0 + (B - 1) * PER
            batch(B - 1, False, xflat[:, (B - 1) * TB * D:B * TB * D])

            for hf in range(2):
                layernorm(1, hf, lambda t: dve.wait_ge(x1_ok, B))
            for hf in range(2):
                for n in range(8 * hf, 8 * hf + 8):
                    dve.wait_ge(xp_sg, n + 1)
                    if n >= 2:
                        dve.wait_ge(xa_ok, n - 1)
                    dve.tensor_tensor(pm[:, n % 2, :], ps_t[(n % 4) // 2][:, (n % 2) * 512:(n % 2 + 1) * 512],
                                      sg[:, n % 2, :], ALU.mult).then_inc(xp_pm, 1)
                for t in range(hf * TH, hf * TH + TH):
                    dve.wait_ge(xy_ps, t + 1)
                    dve.tensor_tensor(xs[:, t, :], ps_s[t % 2][:, 0:D], xs[:, t, :], ALU.add).then_inc(x2_ok, 1)
            for hf in range(2):
                layernorm(2, hf, lambda t: dve.wait_ge(x2_ok, TT))
            dve.wait_ge(lg_ps, 1)
            mine.done(dve.tensor_copy(lg[:], ps_o[:, 0:TT * E].rearrange("p (t e) -> p t e", t=TT)))
            mine.wait()
            for t in range(TT):
                mine.done(dve.max(mx8[:, t, :], lg[:, t, :]))
            mine.wait()
            for t in range(TT):
                mine.done(dve.max_index(ix8[:, t, :], mx8[:, t, :], lg[:, t, :]))
            dve.tensor_tensor(gw[:, 0, :], mx8[:, :, 1], mx8[:, :, 0], ALU.subtract).then_inc(gd_ok, 1)
            mine.wait()
            mine.done(dve.tensor_copy(ixf[:], ix8[:, :, 0:2]))
            mine.wait()
            for r in range(2):
                mine.done(dve.tensor_tensor(oh[:, r, :, :], iota[:].unsqueeze(1).broadcast_to([P, TT, E]),
                                            ixf[:, :, r:r + 1].broadcast_to([P, TT, E]), ALU.is_equal))
            mine.wait()
            dve.tensor_tensor(chosen[:], oh[:, 0, :, :], oh[:, 1, :, :], ALU.add).then_inc(ch_ok, 1)
            dve.wait_ge(ge_ok, 1)
            mine.done(dve.tensor_scalar(gw[:, 2, :], gw[:, 1, :], 1.0, None, ALU.add))
            mine.wait()
            mine.done(dve.reciprocal(gw[:, 3, :], gw[:, 2, :]))
            mine.wait()
            mine.done(dve.tensor_tensor(gw[:, 0, :], gw[:, 3, :], gw[:, 1, :], ALU.mult))

            def shared_mult(hf, fs):
                for f in fs:
                    m = FS * hf + f
                    dve.wait_ge(gu_sg, m + 1)
                    if hf == 1:
                        dve.wait_ge(gy_ps, TH)
                    dve.tensor_tensor(aT[:, f, :], ps_t[m % 2][:, 512:1024], sg[:, m % 2, :], ALU.mult).then_inc(ga_ok, 1)

            def shared_add(hf):
                for t in range(hf * TH, hf * TH + TH):
                    dve.wait_ge(gy_ps, t + 1)
                    dve.tensor_tensor(xs[:, t, :], ps_s[t % 2][:, 0:D], xs[:, t, :], ALU.add).then_inc(gy_ok, 1)

            shared_mult(0, range(0, 2))
            dve.wait_ge(rk_ps, 1)
            dve.wait_ge(ld_lt, 32)
            n_i, n_t, n_f, ends, starts, ones8 = (cnt[:, i, :] for i in range(6))
            mine.done(dve.tensor_scalar(n_i.bitcast(I32), ps_m[:, TT * E:TT * E + E], float(P - 1), None, ALU.add))
            mine.done(dve.memset(ones8, 1.0))
            mine.wait()
            mine.done(dve.tensor_scalar(n_t.bitcast(I32), n_i.bitcast(I32), 7, None, ALU.logical_shift_right))
            mine.wait()
            mine.done(dve.tensor_copy(n_f, n_t.bitcast(I32)))
            mine.wait()
            mine.done(dve.tensor_tensor_scan(ends, ones8, n_f, 0.0, ALU.mult, ALU.add))
            mine.wait()
            mine.done(dve.tensor_tensor(starts, ends, n_f, ALU.subtract))
            mine.done(dve.tensor_tensor(tge[:], tiles[:], ends[0:1, 0:E - 1].unsqueeze(1).broadcast_to([1, NM, E - 1]), ALU.is_ge))
            mine.wait()
            mine.done(dve.scalar_tensor_tensor(out=posf[:], in0=starts.unsqueeze(1).broadcast_to([P, TT, E]),
                                               scalar=float(P), in1=ps_m[:, 0:TT * E].rearrange("p (t e) -> p t e", t=TT),
                                               op0=ALU.mult, op1=ALU.add))
            mine.done(dve.tensor_reduce(eidf[:], tge[:], AXX, ALU.add))
            mine.wait()
            dve.tensor_copy(eid[:], eidf[:]).then_inc(eid_ok, 1)
            for r in range(2):
                mine.done(dve.tensor_tensor(posm[:, r, :, :], oh[:, r, :, :], posf[:], ALU.mult))
            mine.wait()
            mine.done(dve.tensor_reduce(posr[:], posm[:], AXX, ALU.add))
            mine.wait()
            dve.tensor_copy(pos[:], posr[:].rearrange("p r t -> p (r t)")).then_inc(pos_ok, 1)
            shared_mult(0, range(2, FS))
            shared_add(0)
            dve.sem_inc(ma_ok, 2)
            dve.sem_inc(my_sb, 2)

            def tile_mult(i, par):
                dve.wait_ge(m_sg, i + 1)
                dve.wait_ge(mu_ps, i + 3)
                dve.wait_ge(at_ps, i + 1)
                dve.tensor_tensor(ma[:, par, :], ps_t[par][:, 512:1024], msg[:, par, :], ALU.mult).then_inc(ma_ok, 1)

            def tile_out(i, par, stored):
                dve.wait_ge(my_ps, i + 3)
                if stored is not None:
                    dve.wait_ge(y_out[par], stored)
                dve.tensor_copy(ysb[:, par, :], ps_s[par][:, 0:D]).then_inc(my_sb, 1)

            tile_mult(0, 0)
            tile_mult(1, 1)
            tile_out(0, 0, None)
            tile_mult(2, 0)
            tile_out(1, 1, None)
            with dve.Fori(1, NM // 2) as j:
                for par in range(2):
                    i = 2 * j + par
                    tile_mult(i + 1, 1 - par)
                    tile_out(i, par, 16 * j)
            tile_out(NM - 1, 0, 16 * (NM // 2))
            shared_mult(1, range(FS))
            for hf in range(2):
                dve.wait_ge(gath[hf], 32 * TH)
                for t in range(hf * TH, hf * TH + TH):
                    dve.wait_ge(gy_ok, TH)
                    for r, w in ((0, 3), (1, 0)):
                        ins = dve.scalar_tensor_tensor(out=xs[:, t, :], in0=gat[:, r, t, :], scalar=gw[:, w, t:t + 1],
                                                       in1=xs[:, t, :], op0=ALU.mult, op1=ALU.add)
                        if r == 0:
                            mine.done(ins)
                            mine.wait()
                    if hf == 0:
                        ins.then_inc(fin_ok, 1)
                    else:
                        mine.done(ins)
                        mine.wait()
            for t in range(TH, TT):
                dve.wait_ge(gy_ps, t + 1)
                dve.tensor_tensor(xs[:, t, :], ps_s[t % 2][:, 0:D], xs[:, t, :], ALU.add).then_inc(fin_ok, 1)

        @block.tensor
        def _(pe):
            def transposes(stage, hf, banks):
                for k in range(KD):
                    pe.wait_ge(h_ready, 8 * stage + TH * (hf + 1))
                    n = 4 * stage + 2 * hf + k
                    if n >= 2:
                        pe.wait_ge(hT_sb, n - 1)
                    for t in range(TH):
                        last = pe.transpose(banks[k][:, t * P:(t + 1) * P], hn[:, hf * TH + t, k * P:(k + 1) * P], ident[:])
                    last.then_inc(hT_ps, 1)

            pe.sem_inc(pv_done, 2)
            pe.sem_inc(xT_ps, 2)
            pe.sem_inc(mu_ps, 2)
            pe.sem_inc(my_ps, 2)
            pe.sem_inc(at_ps, 2)

            pe.wait_ge(ld_wqk, 32)
            for hf in range(2):
                tok = slice(hf * HALF, (hf + 1) * HALF)
                transposes(0, hf, ps_s)
                pe.wait_ge(hT_sb, 2 * hf + 2)
                for n in range(4 * hf, 4 * hf + 4):
                    if hf == 1:
                        pe.wait_ge(qk_h, n - 3)
                    bank = ps_t[(n % 4) // 2][:, (n % 2) * 512:(n % 2 + 1) * 512]
                    for k in range(KD):
                        last = pe.matmul(bank, wqk[:, k, (n % 4) * P:(n % 4 + 1) * P], hT[:, k, tok],
                                         start=(k == 0), stop=(k == KD - 1))
                    last.then_inc(qk_ps, 1)
                if hf == 0:
                    pe.wait_ge(ld_wv, 16)
                for i, bank in enumerate((ps_o, ps_m)):
                    if hf == 1:
                        pe.wait_ge(v_sb, i + 1)
                    for t in range(2):
                        tt = hf * TH + 2 * i + t
                        for k in range(KD):
                            last = pe.matmul(bank[:, t * D:(t + 1) * D], hT[:, k, tt * P:(tt + 1) * P], wv[:, k, :],
                                             start=(k == 0), stop=(k == KD - 1))
                    last.then_inc(v_ps, 1)

            def scores(n, h, rows, keys):
                pe.wait_ge(s_used, n + 1)
                for tt in range(TB):
                    last = pe.matmul(ps_s[h % 2][:, tt * S:(tt + 1) * S], rows(h, tt), keys(h), start=True, stop=True)
                last.then_inc(s_ready, 1)

            def rows_of(b):
                return (lambda h, tt: qst[0:KS_ROWS, h, bass.ds(b * S + tt * P, P)],
                        lambda h: kst[0:KS_ROWS, h, bass.ds(b * S, S)])

            def max_rows(b):
                pe.wait_ge(s_used, 16 * b + 18)
                pe.transpose(ps_m[0:2 * H, 0:P], rmax[:, :, :].rearrange("p t h -> p (t h)"), ident[:]).then_inc(rm_T, 1)

            def batch(b, more):
                def exps_in(i):
                    q, st = i // 2, i % 2
                    pe.wait_ge(p_ready, 8 * b + i + 1)
                    for j in range(Q4):
                        h = Q4 * q + j
                        last = pe.matmul(ps_t[i % 2][:, j * S:(j + 1) * S], kst[0:KA_ROWS, h, bass.ds(b * S + st * P, P)],
                                         qst[0:KA_ROWS, h, bass.ds(b * S, S)], start=True, stop=True)
                    last.then_inc(t_ready, 1)

                def values(i):
                    q, st = i // 2, i % 2
                    pe.wait_ge(p_ready, 8 * b + i + 3)
                    if st == 0:
                        pe.wait_ge(o_evac, 4 * b + q + 1)
                    for j in range(Q4):
                        h = Q4 * q + j
                        last = pe.matmul(ps_o[HP * j:HP * (j + 1), 0:S], vaug[:, st, h, :], pt[:, i % 2, j * S:(j + 1) * S],
                                         start=(st == 0), stop=(st == TB - 1))
                    last.then_inc(pv_done, 1)

                def sums(q):
                    pe.wait_ge(o_evac, 4 * b + q + 2)
                    if q > 0:
                        pe.wait_ge(on_ready, 4 * b + q + 4)
                    if q == 2 and more:
                        pe.wait_ge(nm_ready, b + 2)
                    pe.matmul(ps_m[:, 0:S], sel[:], osb[:, q, :], start=True, stop=True).then_inc(bc_ready, 1)

                pe.wait_ge(aug_in, 32 * b + 32)
                pe.wait_ge(vaug_ok, b + 1)
                exps_in(0)
                h = 0
                for i in range(8):
                    if i < 7:
                        exps_in(i + 1)
                    if more:
                        rows, keys = rows_of(b + 1)
                        for _ in range(S_IN_SLOT[i]):
                            scores(16 * b + 16 + h, h, rows, keys)
                            h += 1
                    values(i)
                    if i in (3, 5, 7):
                        sums((i - 3) // 2)
                    if i == 6 and more:
                        pe.wait_ge(on_ready, 4 * b + 6)
                        max_rows(b + 1)
                sums(NQ - 1)
                pe.wait_ge(on_ready, 4 * b + 8)
                for tt in range(TB):
                    for q in range(NQ):
                        last = pe.matmul(ps_m[:, tt * D:(tt + 1) * D], onm[:, q, tt * P:(tt + 1) * P], wp[:, q, :],
                                         start=(q == 0), stop=(q == NQ - 1))
                last.then_inc(pr_ready, 1)
                pe.wait_ge(x1_ok, b + 1)

            pe.wait_ge(qk_in[0], 192)
            rows, keys = rows_of(0)
            for h in range(H):
                scores(h, h, lambda h, tt: qst[0:KS_ROWS, h, tt * P:(tt + 1) * P], lambda h: kst[0:KS_ROWS, h, 0:S])
            pe.wait_ge(v_sb, 4)
            max_rows(0)
            pe.wait_ge(qk_in[1], 192)
            pe.wait_ge(qk_h, 8)
            pe.wait_ge(s_const, 2)
            pe.wait_ge(ld_wp, 16)
            pe.wait_ge(ld_c, 64)
            pe.wait_ge(nm_ready, 1)
            with pe.Fori(0, B - 1) as b:
                batch(b, True)
            batch(B - 1, False)

            for hf in range(2):
                transposes(1, hf, (ps_o, ps_m))
            pe.wait_ge(ld_ct, 16)
            pe.wait_ge(p_ready, 8 * B + 2)
            for hf in range(2):
                tok = slice(hf * HALF, (hf + 1) * HALF)
                pe.wait_ge(hT_sb, 4 + 2 * hf + 2)
                for n in range(8 * hf, 8 * hf + 8):
                    e, fb = (n % 8) // 2, n % 2
                    if n >= 4:
                        pe.wait_ge(xp_pm, n - 3)
                    bank = ps_t[(n % 4) // 2][:, (n % 2) * 512:(n % 2 + 1) * 512]
                    for k in range(KD):
                        last = pe.matmul(bank, ct[:, e, k, fb * P:(fb + 1) * P], hT[:, k, tok],
                                         start=(k == 0), stop=(k == KD - 1))
                    last.then_inc(xp_ps, 1)
                for t in range(TH):
                    tt = hf * TH + t
                    pe.wait_ge(xa_ok, 8 * hf + 8)
                    if tt >= 2:
                        pe.wait_ge(x2_ok, tt - 1)
                    for i in range(8):
                        last = pe.matmul(ps_s[tt % 2][:, 0:D], aT[:, i, t * P:(t + 1) * P], ct[:, i // 2, i % 2, :],
                                         start=(i == 0), stop=(i == 7))
                    last.then_inc(xy_ps, 1)
            for hf in range(2):
                transposes(2, hf, (ps_o, ps_m))
            pe.wait_ge(ld_rw, 16)
            pe.wait_ge(hT_sb, 12)
            for tt in range(TT):
                for k in range(KD):
                    last = pe.matmul(ps_o[:, tt * E:(tt + 1) * E], hT[:, k, tt * P:(tt + 1) * P], rw[:, k, :],
                                     start=(k == 0), stop=(k == KD - 1))
            last.then_inc(lg_ps, 1)

            def shared_up(hf, fs):
                tok = slice(hf * HALF, (hf + 1) * HALF)
                for f in fs:
                    m = FS * hf + f
                    if m >= 2:
                        pe.wait_ge(ga_ok, m - 1)
                    for o in range(2):
                        for k in range(KD):
                            last = pe.matmul(ps_t[m % 2][:, o * 512:(o + 1) * 512], wsg[:, o, k, f * P:(f + 1) * P],
                                             hT[:, k, tok], start=(k == 0), stop=(k == KD - 1))
                    last.then_inc(gu_ps, 1)

            def shared_down(hf):
                pe.wait_ge(ga_ok, FS * (hf + 1))
                for t in range(TH):
                    tt = hf * TH + t
                    if t >= 2:
                        pe.wait_ge((gy_ok, fin_ok)[hf], tt - 1)
                    for f in range(FS):
                        last = pe.matmul(ps_s[tt % 2][:, 0:D], aT[:, f, t * P:(t + 1) * P], wsd[:, f, :],
                                         start=(f == 0), stop=(f == FS - 1))
                    last.then_inc(gy_ps, 1)

            pe.wait_ge(x2_ok, TT)
            pe.wait_ge(xp_pm, 16)
            pe.wait_ge(ld_ws, 48)
            shared_up(0, range(0, 2))
            pe.wait_ge(ch_ok, 1)
            pe.wait_ge(lt_ok, 2)
            pe.matmul(ps_m[:, 0:TT * E], beforeb[:], chosen[:].rearrange("p t e -> p (t e)"), start=True, stop=False,
                      skip_group_check=True)
            for t in range(TT - 1):
                later = TT - 1 - t
                pe.matmul(ps_m[:, (t + 1) * E:TT * E], onesb[:], chosen[:, t:t + 1, :].broadcast_to([P, later, E]),
                          start=False, stop=False, skip_group_check=True)
            for t in range(TT):
                last = pe.matmul(ps_m[:, TT * E:TT * E + E], onesb[:], chosen[:, t, :], start=False, stop=(t == TT - 1),
                                 skip_group_check=True)
            last.then_inc(rk_ps, 1)
            shared_up(0, range(2, FS))
            shared_down(0)

            def expert_of(i):
                return pe.value_load(eid[0:1, bass.ds(i, 1)], min_val=0, max_val=E - 1)

            def turn_rows(i, par, loads):
                pe.wait_ge(ld_xt[par], loads)
                pe.wait_ge(xT_sb, i) if not isinstance(i, int) or i > 0 else None
                for k in range(KD):
                    last = pe.transpose(ps_o[:, k * P:(k + 1) * P], xt[:, par, k * P:(k + 1) * P], ident[:])
                last.then_inc(xT_ps, 1)

            def up(i, par):
                e = expert_of(i)
                pe.wait_ge(xT_sb, i + 1)
                pe.wait_ge(ma_ok, i + 1)
                for o, done in ((0, mg_ps), (1, mu_ps)):
                    for k in range(KD):
                        last = pe.matmul(ps_t[par][:, o * 512:(o + 1) * 512], xtT[:, par, k * P:(k + 1) * P],
                                         big[:, bass.ds(e * W1S + (2 * k + o) * INTER, INTER)],
                                         start=(k == 0), stop=(k == KD - 1))
                    last.then_inc(done, 1)

            def turn_hidden(i, par):
                pe.wait_ge(ma_ok, i + 3)
                pe.wait_ge(at_sb, i) if not isinstance(i, int) or i > 0 else None
                for f in range(FB):
                    last = pe.transpose(ps_m[:, f * P:(f + 1) * P], ma[:, par, f * P:(f + 1) * P], ident[:])
                last.then_inc(at_ps, 1)

            def down(i, par):
                e = expert_of(i)
                pe.wait_ge(at_sb, i + 1)
                pe.wait_ge(my_sb, i + 1)
                for f in range(FB):
                    last = pe.matmul(ps_s[par][:, 0:D], maT[:, par, f * P:(f + 1) * P],
                                     big[:, bass.ds(e * W2S + W2O + f * D, D)], start=(f == 0), stop=(f == FB - 1))
                last.then_inc(my_ps, 1)

            pe.wait_ge(eid_ok, 1)
            pe.wait_ge(ld_we, 16 * 2 * E)
            pe.wait_ge(gy_ok, TH)
            turn_rows(0, 0, 16)
            up(0, 0)
            with pe.Fori(0, NM // 2) as j:
                for par in range(2):
                    i = 2 * j + par
                    turn_rows(i + 1, 1 - par, 16 * j + 16 * (par + 1))
                    turn_hidden(i, par)
                    up(i + 1, 1 - par)
                    down(i, par)
            turn_hidden(NM - 1, 0)
            down(NM - 1, 0)
            pe.wait_ge(ma_ok, NM + 2)
            pe.wait_ge(my_sb, NM + 2)
            shared_up(1, range(FS))
            shared_down(1)


def _consts():
    p = np.arange(P)
    ident = np.eye(P, dtype=np.float32)
    sel = (p[:, None] == (p[None, :] // HP) * HP + HD).astype(np.float32)
    first = (p % HD) < HD // 2
    coef = np.stack([np.where(first, SCALE, 0.0), np.where(first, 0.0, -SCALE)], axis=1).astype(np.float32)
    iota = np.tile(np.arange(E, dtype=np.float32), (P, 1))
    before = (p[:, None] < p[None, :]).astype(np.float32)
    tiles = np.repeat(np.arange(NM, dtype=np.float32)[:, None], E - 1, axis=1)[None]
    return {"ident": ident, "sel": sel, "coef": coef, "iota": iota, "before": before, "tiles": tiles}


def kernel(x, itok_BxS_13_99985, ctx_2048, L0_attn_W_attn, L0_attn_W_proj, L0_attn_lambda_q1, L0_attn_lambda_k1,
           L0_attn_lambda_q2, L0_attn_lambda_k2, L0_ffn_router_w, L0_ffn_w1, L0_ffn_w2, L0_ffn_w_gate, L0_ffn_w_up,
           L0_ffn_w_down):
    import concourse.bacc as _bacc
    from concourse.bass_utils import run_bass_kernel_spmd as _run

    C = D // 2
    w = np.asarray(L0_attn_W_attn)
    q1, k1, q2, k2 = (w[:, i * C:(i + 1) * C].reshape(D, H, HD // 2) for i in range(4))
    wq = np.concatenate([q1, q2], axis=2).reshape(D, D)
    wk = np.concatenate([k1, k2], axis=2).reshape(D, D)
    wqk = np.concatenate([wq, wk], axis=1).reshape(KD, P, 2 * D).transpose(1, 0, 2)
    wv = w[:, 4 * C:].reshape(KD, P, D).transpose(1, 0, 2)
    wp = np.zeros((NQ, Q4, HP, D), np.float32)
    wp[:, :, :HD, :] = np.asarray(L0_attn_W_proj).reshape(NQ, Q4, HD, D)
    wp = wp.reshape(NQ, P, D).transpose(1, 0, 2)
    ctxT = np.asarray(ctx_2048).transpose(2, 0, 1).reshape(KD, P, XE, D).transpose(1, 2, 0, 3)
    lam_vecs = np.stack([np.asarray(L0_attn_lambda_q1), np.asarray(L0_attn_lambda_k1),
                         np.asarray(L0_attn_lambda_q2), np.asarray(L0_attn_lambda_k2)])
    c = _consts()
    arrays = {
        "x": x, "ids": np.asarray(itok_BxS_13_99985).reshape(T), "ctxT": ctxT, "w_qk": wqk, "w_v": wv, "w_proj": wp,
        "lam_vecs": lam_vecs, "router_w": L0_ffn_router_w, "w1": L0_ffn_w1, "w2": L0_ffn_w2,
        "w_gate": L0_ffn_w_gate, "w_up": L0_ffn_w_up, "w_down": L0_ffn_w_down,
        "ident_c": c["ident"], "sel_c": c["sel"], "coef_c": c["coef"], "iota_c": c["iota"],
        "before_c": c["before"], "tiles_c": c["tiles"],
    }
    nc = _bacc.Bacc("TRN2", target_bir_lowering=False, num_devices=1)
    feeds, args = {}, []
    for name, a in arrays.items():
        a = np.ascontiguousarray(a)
        feeds[f"in_{name}"] = a
        args.append(nc.dram_tensor(f"in_{name}", a.shape, mybir.dt.from_np(a.dtype), kind="ExternalInput").ap())
    args.append(nc.dram_tensor("out_0", (B, S, D), F32, kind="ExternalOutput").ap())
    decoder_layer(nc, *args)
    r = _run(nc, [feeds], core_ids=[0])
    return r.results[0]["out_0"]
```

```python
from contextlib import ExitStack

import numpy as np

import concourse.bass as bass
from concourse import mybir

F32 = mybir.dt.float32
F32R = mybir.dt.float32r
BF16 = mybir.dt.bfloat16
I32 = mybir.dt.int32
U32 = mybir.dt.uint32
ALU = mybir.AluOpType
ACT = mybir.ActivationFunctionType
AXX = mybir.AxisListType.X

P = 128
B, S, D = 4, 256, 256
T = B * S
TT = T // P
TB = S // P
HALF = T // 2
TH = HALF // P
KD = D // P
H = 16
HD = D // H
HP = 32
Q4 = 4
NQ = H // Q4
LAMBDA_INIT = 0.2
SCALE = float(HD // 2) ** -0.5
EPS = 1e-5
Q_PARTS = (0, 0, 1, 0, 2, 1)
K_PARTS = (0, 1, 0, 2, 0, 1)
NT = len(Q_PARTS)
PIECES = (((0, S), (S, HALF)), ((HALF, T),))
KS_ROWS = NT * HD
KA_ROWS = KS_ROWS + 3
XE = 4
VOCAB = 12500
PER_X = VOCAB // XE
E = 8
INTER = 512
SHARED = 1024
NM = (T * 2 + E * (P - 1)) // P
MAGIC = float(0x5F3759DF)

HEADS_IN_SLOT = (2, 2, 1, 1, 2, 1, 2, 1)
HEADS_AT_END = (2, 2)
X_PIECES = ((0, 2), (2, TH), (TH, TT))
OUT_PIECES = ((0, TH), (TH, TT - 1), (TT - 1, TT))
SBUF_FROM, SBUF_TO = 16512, 229344
HIGH_LAG, LOW_LAG, DOWN_LAG = 2, 3, 5
WARM_UP = 3


def decoder_layer(nc, x, ids, ctxT, w_qk, w_v, w_proj, lam_vecs, router_w, w1, w2, w_gate, w_up, w_down,
                  ident_c, coef_c, iota_c, before_c, tiles_c, out):
    with ExitStack() as ctx:
        places, free = {}, [SBUF_FROM]

        def sb(name, shape, dt=F32, over=None):
            if over is None:
                places[name] = free[0]
                free[0] += -(-int(np.prod(shape[1:])) * mybir.dt.size(dt) // 32) * 32
                assert free[0] <= SBUF_TO
            else:
                places[name] = places[over[0]] + 4 * over[1]
            return nc.alloc_sbuf_tensor_at(name, shape, dt, offset=places[name], align_bytes=32)

        def sem(name):
            return ctx.enter_context(nc.semaphore(name))

        xs = sb("xs", [P, TT, D])
        hn = sb("hn", [P, TT, D])
        hT = sb("hT", [P, KD, T])
        st6 = sb("st6", [P, TT, 6])
        mv = sb("mv", [P, TT, 2])
        nw = sb("nw", [P, 6, TT])
        weights_place = sb("weights_place", [P, 6144])
        w_qk_sb = weights_place[:, 0:1024].rearrange("p (k n) -> p k n", k=KD)
        w_v_sb = weights_place[:, 1024:1536].rearrange("p (k n) -> p k n", k=KD)
        w_proj_sb = weights_place[:, 1536:2048].rearrange("p (k n) -> p k n", k=KD)
        qk_f32 = weights_place[:, 2560:3584].rearrange("p (s t) -> p s t", s=2)
        qk_rest = weights_place[:, 3584:4608].rearrange("p (s t) -> p s t", s=2)
        ids_f = weights_place[:, 4608:5632]
        shared_gu = weights_place[:, 0:4096].rearrange("p (o k f) -> p o k f", o=2, k=KD)
        shared_d = weights_place[:, 4096:6144].rearrange("p (k n) -> p k n", k=SHARED // P)
        ident = sb("ident", [P, P])
        coefc = sb("coefc", [P, 2])
        early_place = sb("early_place", [P, 2048])
        lamv = early_place[:, 0:1024].rearrange("p (v d) -> p v d", v=4)
        ids_ge = early_place[:, 1024:2048].bitcast(BF16).rearrange("p (s t) -> p s t", s=2)
        lam = sb("lam", [P, 8])
        coef = sb("coef", [P, 1])
        big_place = sb("big_place", [P, 24576])
        q_rows = big_place[:, 0:8192].bitcast(BF16).rearrange("p (h t) -> p h t", h=H)
        k_rows = big_place[:, 8192:16384].bitcast(BF16).rearrange("p (h t) -> p h t", h=H)
        values_all = big_place[:, 16384:18432].rearrange("p (t h d) -> p t h d", t=TT, h=H)
        values_1 = big_place[:, 18432:19456].rearrange("p (t h d) -> p t h d", t=TB, h=H)
        probs = big_place[:, 19456:21504].rearrange("p (s n) -> p s n", s=2)
        out_sb = big_place[:, 21504:22528].rearrange("p (q t) -> p q t", q=NQ)
        out_n = big_place[:, 22528:23040].rearrange("p (t h d) -> p t h d", t=TB, h=H)
        out_T = big_place[:, 23040:23552].rearrange("p (t k n) -> p t k n", t=TB, k=KD)
        W1S, W2S, W2O = KD * 2 * INTER, INTER // P * D, E * KD * 2 * INTER
        sum_inv = sb("sum_inv", [P, TB, Q4])
        middle_place = sb("middle_place", [P, 6144])
        parts = middle_place[:, :].bitcast(BF16).rearrange("p (w j b t) -> p w j b t", w=2, j=3, b=2)
        row_max = sb("row_max", [P, TB, H])
        minus_max_f = sb("minus_max_f", [2 * H, 2, P])
        minus_max_p = sb("minus_max_p", [2 * H, 3, P], BF16)
        ctx_w = sb("ctx_w", [P, XE, KD, D])
        tile_place = sb("tile_place", [P, 3584])
        xmask = tile_place[:, 0:2048].bitcast(BF16).rearrange("p (e t) -> p e t", e=XE)
        tile_x = tile_place[:, 0:512].rearrange("p (s d) -> p s d", s=2)
        tile_xT = tile_place[:, 512:1024].rearrange("p (s t) -> p s t", s=2)
        units = tile_place[:, 1024:2048].rearrange("p (s f) -> p s f", s=2)
        unitsT = tile_place[:, 2048:3072].rearrange("p (s f) -> p s f", s=2)
        tile_y = tile_place[:, 3072:3584].rearrange("p (s d) -> p s d", s=2)
        ids_i = tile_place[:, 2048:3072].bitcast(I32)
        hTh = sb("hTh", [P, KD, T], F32R, over=("hT", 0))
        hTl = sb("hTl", [P, KD, T], F32R, over=("early_place", 0))
        ctx_h = sb("ctx_h", [P, XE, KD, D], F32R, over=("middle_place", 0))
        ctx_l = sb("ctx_l", [P, XE, KD, D], F32R, over=("middle_place", 2048))
        voc_Th = sb("voc_Th", [P, XE * KD, HALF], F32R, over=("big_place", W2O))
        voc_Tl = sb("voc_Tl", [P, XE * KD, HALF], F32R, over=("big_place", W2O + 4096))
        router = sb("router", [P, KD, E])
        router_h = sb("router_h", [P, KD, E], F32R)
        router_l = sb("router_l", [P, KD, E], F32R)
        shared_gu_h = [sb("shared_gu_h0", [P, 2, KD, INTER], F32R, over=("tile_place", 1536)),
                       sb("shared_gu_h1", [P, 2, KD, INTER], F32R, over=("ctx_w", 0))]
        shared_gu_l = sb("shared_gu_l", [P, 2, KD, SHARED], F32R, over=("weights_place", 0))
        masked = ctx_w[:, :, :, :].rearrange("p e k d -> p (e k d)").rearrange("p (s t) -> p s t", s=4)
        zrow = sb("zrow", [P, D])
        before = sb("before", [P, P])
        beforeb = sb("beforeb", [P, P], BF16)
        onesb = sb("onesb", [P, P], BF16)
        tiles = sb("tiles", [1, NM, E - 1])
        tile_ge = sb("tile_ge", [1, NM, E - 1])
        eidf = sb("eidf", [1, NM])
        eid = sb("eid", [1, NM], I32)
        chosen = sb("chosen", [P, TT, E], BF16)
        cnt = sb("cnt", [P, 6, E])
        posf = sb("posf", [P, TT, E])
        posm = sb("posm", [P, 2, TT, E])
        posr = sb("posr", [P, 2, TT])
        pos = sb("pos", [P, 2 * TT], U32)
        shared_T = middle_place[:, 0:4096].rearrange("p (f t) -> p f t", f=8)
        silu = middle_place[:, 4096:5120].rearrange("p (s t) -> p s t", s=2)
        hidden_f = middle_place[:, 5120:6144].rearrange("p (s t) -> p s t", s=2)
        tile_silu_sb = hidden_f
        iota = sb("iota", [P, E])
        logits = sb("logits", [P, TT, E])
        logitsT = sb("logitsT", [E, T], over=("tile_place", 0))
        top8 = sb("top8", [P, TT, 8])
        top8_at = sb("top8_at", [P, TT, 8], U32)
        top2_at = sb("top2_at", [P, TT, 2])
        onehot = sb("onehot", [P, 2, TT, E])
        gates = sb("gates", [P, 4, TT])
        w1v = big_place[:, 0:W2O].rearrange("p (e k f) -> p e k f", e=E, k=KD)
        w2v = big_place[:, W2O:W2O + E * W2S].rearrange("p (e k n) -> p e k n", e=E, k=INTER // P)
        gathered = big_place[:, 0:2 * TT * D].rearrange("p (r t d) -> p r t d", r=2, t=TT)

        ps_s = [ctx.enter_context(nc.psum_tensor(f"ps_s{i}", [P, 512], F32)) for i in range(2)]
        ps_t = [ctx.enter_context(nc.psum_tensor(f"ps_t{i}", [P, 1024], F32)) for i in range(2)]
        ps_o = ctx.enter_context(nc.psum_tensor("ps_o", [P, 512], F32))
        ps_m = ctx.enter_context(nc.psum_tensor("ps_m", [P, 512], F32))

        FIRST_S = (ps_s[0], ps_s[1], ps_o)

        qk_dram = nc.dram_tensor("qk_parts", (2, 3, KD, P, T), BF16, kind="Internal").ap()
        xp_dram = nc.dram_tensor("routed_rows", (NM * P, D), F32, kind="Internal").ap()
        yp_dram = nc.dram_tensor("routed_out", (NM * P, D), F32, kind="Internal").ap()
        mx_dram = nc.dram_tensor("mx_parts", (3, TB, H, P), BF16, kind="Internal").ap()

        x_loaded = [sem(f"x_loaded{i}") for i in range(len(X_PIECES))]
        consts_loaded = sem("consts_loaded")
        ids_loaded = sem("ids_loaded")
        ident_loaded = sem("ident_loaded")
        wqk_loaded = sem("wqk_loaded")
        wv_loaded = sem("wv_loaded")
        wproj_loaded = sem("wproj_loaded")
        ctx_loaded = sem("ctx_loaded")
        router_w_loaded = sem("router_w_loaded")
        memsets_done = sem("memsets_done")
        dve_step = sem("dve_step")
        coef_ready = sem("coef_ready")
        lambda_dots = sem("lambda_dots")
        lambda_exps = sem("lambda_exps")
        rows_normalised = sem("rows_normalised")
        hT_product = sem("hT_product")
        hT_copied = sem("hT_copied")
        qk_product = sem("qk_product")
        qk_copied = sem("qk_copied")
        qk_high = sem("qk_high")
        qk_left = sem("qk_left")
        qk_low = sem("qk_low")
        qk_parts_out = [sem(f"qk_parts_out{i}") for i in range(2)]
        qk_parts_in = [sem(f"qk_parts_in{i}") for i in range(3)]
        v_product = sem("v_product")
        v_copied = sem("v_copied")
        scores_ready = sem("scores_ready")
        scores_used = sem("scores_used")
        maxima_turned = sem("maxima_turned")
        minus_max_ready = sem("minus_max_ready")
        max_rows_out = sem("max_rows_out")
        max_rows_in = sem("max_rows_in")
        exponents_ready = sem("exponents_ready")
        weights_ready = sem("weights_ready")
        weighted_done = sem("weighted_done")
        out_copied = sem("out_copied")
        quad_turned = sem("quad_turned")
        batch_turned = sem("batch_turned")
        batch_copied = sem("batch_copied")
        maxima_read = sem("maxima_read")
        quad_normalised = sem("quad_normalised")
        projected = sem("projected")
        values_ready = sem("values_ready")
        attention_added = sem("attention_added")
        masks_ready = sem("masks_ready")
        pool_step = sem("pool_step")
        voc_product = sem("voc_product")
        voc_silu = sem("voc_silu")
        voc_hidden = sem("voc_hidden")
        voc_masked = sem("voc_masked")
        voc_high = sem("voc_high")
        voc_low = sem("voc_low")
        hT_low = sem("hT_low")
        ctx_split = sem("ctx_split")
        router_split = sem("router_split")
        shared_w_high = sem("shared_w_high")
        shared_w_low = sem("shared_w_low")
        voc_out = sem("voc_out")
        voc_added = sem("voc_added")
        logits_turned = sem("logits_turned")
        logits_product = sem("logits_product")
        logits_copied = sem("logits_copied")
        gate_difference = sem("gate_difference")
        gate_exp = sem("gate_exp")
        chosen_ready = sem("chosen_ready")
        ranks_ready = sem("ranks_ready")
        places_ready = sem("places_ready")
        tile_experts_ready = sem("tile_experts_ready")
        counting_ready = sem("counting_ready")
        counting_loaded = sem("counting_loaded")
        shared_w_loaded = sem("shared_w_loaded")
        expert_w_loaded = sem("expert_w_loaded")
        zeros_ready = sem("zeros_ready")
        zeros_out = sem("zeros_out")
        rows_scattered = sem("rows_scattered")
        shared_product = sem("shared_product")
        shared_silu = sem("shared_silu")
        shared_units = sem("shared_units")
        shared_out = sem("shared_out")
        shared_added = sem("shared_added")
        tile_turned = sem("tile_turned")
        tile_copied = sem("tile_copied")
        tile_gates = sem("tile_gates")
        tile_ups = sem("tile_ups")
        tile_gate_silu = sem("tile_gate_silu")
        tile_units = sem("tile_units")
        units_turned = sem("units_turned")
        units_copied = sem("units_copied")
        tile_down = sem("tile_down")
        tile_down_copied = sem("tile_down_copied")
        tile_stored = [sem(f"tile_stored{i}") for i in range(2)]
        result_out = sem("result_out")
        rows_final = sem("rows_final")
        tile_loaded = [sem(f"tile_loaded{i}") for i in range(2)]
        rows_gathered = [sem(f"rows_gathered{i}") for i in range(2)]

        x_rows = x.rearrange("b (s p) d -> p (b s) d", p=P)
        out_rows = out.rearrange("b (s p) d -> p (b s) d", p=P)

        FS, FB = SHARED // P, INTER // P

        block = ctx.enter_context(nc.Block())

        class Steps:

            def __init__(self, eng, s):
                self.eng, self.s, self.n, self.off = eng, s, 0, None

            def done(self, ins):
                self.n += 1
                ins.then_inc(self.s, 1)

            def wait(self):
                self.eng.wait_ge(self.s, self.n if self.off is None else self.off + self.n)

        @block.sync
        def _(sp):
            for i, (t0, t1) in enumerate(X_PIECES):
                sp.dma_start(xs[:, t0:t1, :], x_rows[:, t0:t1, :]).then_inc(x_loaded[i], 16)
            sp.dma_start(lamv[:], lam_vecs.partition_broadcast(P)).then_inc(consts_loaded, 16)
            sp.dma_start(coefc[:], coef_c).then_inc(consts_loaded, 16)
            sp.dma_start(iota[:], iota_c).then_inc(consts_loaded, 16)
            sp.dma_start(before[:], before_c).then_inc(counting_loaded, 16)
            sp.dma_start(tiles[:], tiles_c).then_inc(counting_loaded, 16)
            sp.dma_start(w_proj_sb[:], w_proj).then_inc(wproj_loaded, 16)
            sp.dma_start(ids_i, ids.partition_broadcast(P)).then_inc(ids_loaded, 16)
            sp.dma_start(router[:], router_w.rearrange("(k p) e -> p k e", p=P)).then_inc(router_w_loaded, 16)
            for hf in range(2):
                tok = slice(hf * HALF, (hf + 1) * HALF)
                for w in range(2):
                    sp.wait_ge(qk_high, 4 * hf + 2 * w + 2)
                    sp.wait_ge(qk_low, 4 * hf + 2 * w + 2)
                    for j in range(3):
                        sp.dma_start(qk_dram[w, j, :, :, tok].rearrange("b p t -> p b t"),
                                     parts[:, w, j, :, tok]).then_inc(qk_parts_out[w], 16)
                for piece, (t0, t1) in enumerate(PIECES[hf]):
                    for dst, w, of in ((q_rows, 0, Q_PARTS), (k_rows, 1, K_PARTS)):
                        if piece == 0:
                            sp.wait_ge(qk_parts_out[w], 48 * (hf + 1))
                        for j, part in enumerate(of):
                            src = qk_dram[w, part, :, :, t0:t1].rearrange("b (h d) t -> d (b h) t", d=HD)
                            sp.dma_start(dst[HD * j:HD * (j + 1), :, t0:t1], src).then_inc(qk_parts_in[2 * hf + piece], 16)

            def aug(b):
                sp.wait_ge(minus_max_ready, b + 1)
                sp.dma_start(mx_dram.rearrange("j t h n -> (t h) j n"), minus_max_p[:, :, :]).then_inc(max_rows_out, 16)
                sp.wait_ge(max_rows_out, 16 * b + 16)
                for tt in range(TB):
                    sp.dma_start(q_rows[KS_ROWS:KA_ROWS, :, bass.ds(b * S + tt * P, P)],
                                 mx_dram[:, tt, :, :]).then_inc(max_rows_in, 16)

            for b in range(B):
                if b > 0:
                    sp.wait_ge(max_rows_in, 32 * b)
                aug(b)
                if b == 1:
                    sp.dma_start(ctx_w[:], ctxT).then_inc(ctx_loaded, 16)
                    sp.wait_ge(zeros_ready, 1)
                    sp.dma_start(xp_dram.rearrange("(n p) d -> p n d", p=P),
                                 zrow[:].unsqueeze(1).broadcast_to([P, NM, D])).then_inc(zeros_out, 16)
            sp.wait_ge(attention_added, B + 1)
            sp.wait_ge(masks_ready, 1)
            for o, w in enumerate((w_gate, w_up)):
                sp.dma_start(shared_gu[:, o, :, :], w.rearrange("(k p) f -> p k f", p=P)).then_inc(shared_w_loaded, 16)
            sp.dma_start(shared_d, w_down.rearrange("(k p) n -> p k n", p=P)).then_inc(shared_w_loaded, 16)
            for e in range(E):
                sp.dma_start(w1v[:, e, :, :], w1[e].rearrange("(k p) f -> p k f", p=P)).then_inc(expert_w_loaded, 16)
            sp.wait_ge(voc_out, TT)
            for e in range(E):
                sp.dma_start(w2v[:, e, :, :], w2[e].rearrange("(k p) n -> p k n", p=P)).then_inc(expert_w_loaded, 16)

            def load_rows(i, par):
                sp.wait_ge(tile_turned, i + 1)
                sp.dma_start(tile_x[:, par, :], xp_dram[bass.ds(i * P, P), :]).then_inc(tile_loaded[par], 16)

            sp.wait_ge(rows_scattered, 16 * 2 * TT)
            with sp.Fori(0, NM // 2) as j:
                for par in range(2):
                    load_rows(2 * j + par, par)
            load_rows(NM - 1, 0)
            for t0, t1 in OUT_PIECES:
                sp.wait_ge(rows_final, t1)
                sp.dma_start(out_rows[:, t0:t1, :], xs[:, t0:t1, :]).then_inc(result_out, 16)
            sp.wait_ge(result_out, 16 * len(OUT_PIECES))

        @block.gpsimd
        def _(pool):
            pool.memset(values_1[:, :, :, :], 0.0).then_inc(pool_step, 1)
            pool.wait_ge(pool_step, 1)
            pool.memset(values_1[:, :, :, HD:HD + 1], 1.0).then_inc(memsets_done, 1)
            pool.wait_ge(memsets_done, 1)
            pool.memset(k_rows[KS_ROWS:KA_ROWS, :, :], 1.0).then_inc(memsets_done, 1)
            pool.wait_ge(memsets_done, 2)
            pool.memset(zrow[:], 0.0).then_inc(zeros_ready, 1)
            pool.memset(onesb[:], 1.0).then_inc(counting_ready, 1)
            pool.wait_ge(counting_loaded, 32)
            pool.tensor_copy(beforeb[:], before[:]).then_inc(counting_ready, 1)
            steps = 1
            pool.wait_ge(ids_loaded, 16)
            pool.tensor_copy(ids_f, ids_i).then_inc(pool_step, 1)
            steps += 1
            pool.wait_ge(pool_step, steps)
            for e in range(1, XE):
                a, c = (e - 1) % 2, e % 2
                if e == 1:
                    pool.memset(ids_ge[:, 0, :], 1.0).then_inc(pool_step, 1)
                    steps += 1
                pool.tensor_scalar(ids_ge[:, c, :], ids_f, float(PER_X * e), None, ALU.is_ge).then_inc(pool_step, 1)
                steps += 1
                pool.wait_ge(pool_step, steps)
                pool.tensor_tensor(xmask[:, e - 1, :], ids_ge[:, a, :], ids_ge[:, c, :], ALU.subtract).then_inc(pool_step, 1)
                steps += 1
                pool.wait_ge(pool_step, steps)
                if e == XE - 1:
                    pool.tensor_copy(xmask[:, e, :], ids_ge[:, c, :]).then_inc(masks_ready, 1)

            def vcopy(b, src):
                pool.wait_ge(weighted_done, 8 * b + 2)
                pool.tensor_copy(values_1[:, :, :, 0:HD], src).then_inc(values_ready, 1)

            pool.wait_ge(v_copied, 4)
            pool.wait_ge(memsets_done, 2)
            vcopy(0, values_all[:, 0:TB, :, :])
            pool.wait_ge(ctx_loaded, 16)
            pool.wait_ge(qk_parts_out[0], 96)
            pool.wait_ge(qk_parts_out[1], 96)
            pool.tensor_copy(ctx_h[:, :, :, :], ctx_w[:]).then_inc(ctx_split, 1)
            pool.wait_ge(ctx_split, 1)
            vcopy(1, values_all[:, TB:2 * TB, :, :])
            pool.tensor_tensor(ctx_l[:, :, :, :], ctx_w[:], ctx_h[:, :, :, :].bitcast(F32), ALU.subtract).then_inc(ctx_split, 1)
            pool.wait_ge(router_w_loaded, 16)
            pool.tensor_copy(router_h[:], router[:]).then_inc(router_split, 1)
            pool.wait_ge(router_split, 1)
            pool.tensor_tensor(router_l[:], router[:], router_h[:].bitcast(F32), ALU.subtract).then_inc(router_split, 1)
            with pool.Fori(2, B) as b:
                vcopy(b, values_all[:, bass.ds(b * TB, TB), :, :])
            pool.wait_ge(masks_ready, 1)
            pool.wait_ge(ctx_split, 2)
            for n in range(2 * XE * KD):
                hf, e, fb = n // 8, (n % 8) // 2, n % 2
                pool.wait_ge(voc_hidden, n + 1)
                if n >= 4:
                    pool.wait_ge(voc_high, n - 3)
                    pool.wait_ge(voc_low, n - 3)
                pool.tensor_tensor(masked[:, n % 4, :], hidden_f[:, n % 2, :], xmask[:, e, hf * HALF:(hf + 1) * HALF],
                                   ALU.mult).then_inc(voc_masked, 1)
            for i in range(2):
                pool.wait_ge(shared_w_high, i + 1)
                fs = slice(i * INTER, (i + 1) * INTER)
                pool.tensor_tensor(shared_gu_l[:, :, :, fs].rearrange("p o k f -> p (o k) f"),
                                   shared_gu[:, :, :, fs].rearrange("p o k f -> p (o k) f"),
                                   shared_gu_h[i][:, :, :, :].bitcast(F32).rearrange("p o k f -> p (o k) f"),
                                   ALU.subtract).then_inc(shared_w_low, 1)
            pool.wait_ge(places_ready, 1)
            pool.wait_ge(zeros_out, 16)
            for t in range(TT):
                for r in range(2):
                    pool.indirect_dma_start(out=xp_dram[:, :],
                                            out_offset=bass.IndirectOffsetOnAxis(ap=pos[:, r * TT + t:r * TT + t + 1], axis=0),
                                            in_=hn[:, t, :], in_offset=None).then_inc(rows_scattered, 16)

            def store_rows(i, par):
                pool.wait_ge(tile_down_copied, i + 3)
                pool.dma_start(yp_dram[bass.ds(i * P, P), :], tile_y[:, par, :]).then_inc(tile_stored[par], 16)

            with pool.Fori(0, NM // 2) as j:
                for par in range(2):
                    store_rows(2 * j + par, par)
            store_rows(NM - 1, 0)
            pool.wait_ge(tile_stored[0], 16 * (NM // 2 + 1))
            pool.wait_ge(tile_stored[1], 16 * (NM // 2))
            for t in range(TT):
                for r in range(2):
                    pool.indirect_dma_start(out=gathered[:, r, t, :], out_offset=None, in_=yp_dram[:, :],
                                            in_offset=bass.IndirectOffsetOnAxis(ap=pos[:, r * TT + t:r * TT + t + 1], axis=0),
                                            ).then_inc(rows_gathered[t // TH], 16)

        @block.scalar
        def _(act):
            act.dma_start(ident[:], ident_c).then_inc(ident_loaded, 16)
            act.dma_start(w_qk_sb[:], w_qk).then_inc(wqk_loaded, 16)
            act.dma_start(w_v_sb[:], w_v).then_inc(wv_loaded, 16)
            act.sem_inc(weights_ready, 2)
            act.sem_inc(out_copied, 1)
            act.wait_ge(lambda_dots, 2)
            act.activation(lam[:, 2:4], lam[:, 0:2], ACT.Exp).then_inc(lambda_exps, 1)

            def evac_hT(stage, hf, banks):
                for k in range(KD):
                    n = 4 * stage + 2 * hf + k + 1
                    act.wait_ge(hT_product, n)
                    act.activation((hT if stage == 0 else hTh)[:, k, hf * HALF:(hf + 1) * HALF], banks[k],
                                   ACT.Copy).then_inc(hT_copied, 1)

            for hf in range(2):
                evac_hT(0, hf, (ps_s[0][:], ps_s[1][:]))
                if hf == 0:
                    act.wait_ge(coef_ready, 1)
                for n in range(4 * hf, 4 * hf + 4):
                    w, blk = (n % 4) // 2, n % 2
                    bank = ps_t[(n % 4) // 2][:, (n % 2) * 512:(n % 2 + 1) * 512]
                    act.wait_ge(qk_product, n + 1)
                    if n >= 2:
                        act.wait_ge(qk_left, n - 1)
                    sc = coef[:, 0:1] if w == 0 else 1.0
                    act.activation(qk_f32[:, n % 2, :], bank, ACT.Copy, scale=sc).then_inc(qk_copied, 1)
                    act.activation(parts[:, w, 0, blk, hf * HALF:(hf + 1) * HALF], bank, ACT.Copy, scale=sc).then_inc(qk_high, 1)
                for i, bank in enumerate((ps_o, ps_m)):
                    t = hf * TH + 2 * i
                    act.wait_ge(v_product, 2 * hf + i + 1)
                    act.activation(values_all[:, t:t + 2, :, :], bank[:].rearrange("p (t h d) -> p t h d", t=2, h=H),
                                   ACT.Copy).then_inc(v_copied, 1)

            def weights(b, i):
                act.wait_ge(exponents_ready, 8 * b + i + 1)
                act.wait_ge(weighted_done, 8 * b + i + 1)
                act.activation(probs[:, i % 2, :], ps_t[i % 2][:], ACT.Exp).then_inc(weights_ready, 1)

            def batch(b, following):
                for i in range(2, 8):
                    weights(b, i)
                    if i % 2 == 0 or i == 7:
                        q = i // 2 - 1 if i < 7 else NQ - 1
                        act.wait_ge(weighted_done, 8 * b + 2 * q + 4)
                        act.wait_ge(quad_turned, 4 * b + q + 1)
                        act.activation(out_sb[:, q, :], ps_o[:, 0:S], ACT.Copy).then_inc(out_copied, 1)
                for i in range(2):
                    following(i)
                act.wait_ge(batch_turned, b + 2)
                act.activation(out_T.rearrange("p t k n -> p (t k n)"), ps_m[:], ACT.Copy).then_inc(batch_copied, 1)

            for i in range(2):
                weights(0, i)
            with act.Fori(0, B - 1) as b:
                batch(b, lambda i: weights(b + 1, i))

            def hidden_silu(n):
                act.wait_ge(voc_product, n + 1)
                if n >= 2:
                    act.wait_ge(voc_hidden, n - 1)
                act.activation(silu[:, n % 2, :], ps_t[(n % 4) // 2][:, (n % 2) * 512:(n % 2 + 1) * 512],
                               ACT.Silu).then_inc(voc_silu, 1)

            evac_hT(1, 0, (ps_s[0][:], ps_s[1][:]))
            batch(B - 1, hidden_silu)

            LB = (ps_o[:], ps_m[:])
            def hidden_high(n):
                act.wait_ge(voc_masked, n + 1)
                if n == 0:
                    act.wait_ge(weighted_done, 8 * B + 2)
                if n == 8:
                    act.wait_ge(voc_out, TH)
                act.activation(voc_Th[:, n % 8, :], masked[:, n % 4, :], ACT.Copy).then_inc(voc_high, 1)

            for hf in range(2):
                for n in range(8 * hf, 8 * hf + 8 + HIGH_LAG):
                    if 2 <= n < 8 * hf + 8:
                        hidden_silu(n)
                    if n >= 8 * hf + HIGH_LAG:
                        hidden_high(n - HIGH_LAG)
                if hf == 0:
                    evac_hT(1, 1, LB)

            def weights_high(i):
                act.wait_ge(shared_w_loaded, 48)
                act.wait_ge((voc_masked, voc_low)[i], 2 * XE * KD)
                act.activation(shared_gu_h[i][:, :, :, :].rearrange("p o k f -> p (o k) f"),
                               shared_gu[:, :, :, i * INTER:(i + 1) * INTER].rearrange("p o k f -> p (o k) f"),
                               ACT.Copy).then_inc(shared_w_high, 1)

            weights_high(0)
            evac_hT(2, 0, LB)
            weights_high(1)

            def shared_act(hf, fs):
                for f in fs:
                    m = FS * hf + f
                    act.wait_ge(shared_product, m + 1)
                    if m >= 2:
                        act.wait_ge(shared_units, m - 1)
                    act.activation(silu[:, m % 2, :], ps_t[m % 2][:, 0:512], ACT.Silu).then_inc(shared_silu, 1)

            def tile_in(i, par):
                act.wait_ge(tile_turned, i + 3)
                act.wait_ge(tile_ups, i + 1)
                act.activation(tile_xT[:, par, :], ps_o[:, 0:D], ACT.Copy).then_inc(tile_copied, 1)

            def tile_silu(i, par):
                act.wait_ge(tile_gates, i + 1)
                act.wait_ge(tile_units, i + 1)
                act.activation(tile_silu_sb[:, par, :], ps_t[par][:, 0:INTER], ACT.Silu).then_inc(tile_gate_silu, 1)

            def tile_turn(i, par):
                act.wait_ge(units_turned, i + 3)
                act.wait_ge(tile_down, i + 1)
                act.activation(unitsT[:, par, :], ps_m[:], ACT.Copy).then_inc(units_copied, 1)

            shared_act(0, range(0, 3))
            evac_hT(2, 1, LB)
            for hf, bank in enumerate((ps_o, ps_m)):
                act.wait_ge(logits_product, hf + 1)
                act.activation(logitsT[:, hf * HALF:(hf + 1) * HALF], bank[0:E, :], ACT.Copy).then_inc(logits_copied, 1)
            shared_act(0, range(3, 6))
            act.wait_ge(gate_difference, 1)
            act.activation(gates[:, 1, :], gates[:, 0, :], ACT.Exp).then_inc(gate_exp, 1)
            shared_act(0, range(6, FS))
            shared_act(1, range(0, FS // 2 - 1))
            tile_in(0, 0)
            shared_act(1, range(FS // 2 - 1, FS // 2))
            tile_silu(0, 0)
            with act.Fori(0, NM // 2) as j:
                for par in range(2):
                    i = 2 * j + par
                    tile_in(i + 1, 1 - par)
                    tile_turn(i, par)
                    tile_silu(i + 1, 1 - par)
            tile_turn(NM - 1, 0)
            shared_act(1, range(FS // 2, FS))

        @block.vector
        def _(dve):
            mine = Steps(dve, dve_step)
            dve.sem_inc(scores_used, 2)

            def ln_stats(t0, t1, arrived=lambda t: None):
                for t in range(t0, t1):
                    arrived(t)
                    mine.done(dve.bn_stats(st6[:, t, :], xs[:, t, :]))
                mine.wait()
                for t in range(t0, t1):
                    mine.done(dve.bn_aggr(mv[:, t, :], st6[:, t, :]))

            def ln_root(t0, t1):
                mine.wait()
                ts = slice(t0, t1)
                var, half, y, a, c = (nw[:, i, ts] for i in range(5))
                mine.done(dve.tensor_scalar(var, mv[:, ts, 1], EPS, None, ALU.add))
                mine.wait()
                mine.done(dve.tensor_scalar(half.bitcast(I32), var.bitcast(I32), 1, None, ALU.logical_shift_right))
                mine.wait()
                mine.done(dve.tensor_scalar(y.bitcast(I32), half.bitcast(I32), -1.0, MAGIC, ALU.mult, ALU.add))
                mine.wait()
                for _ in range(3):
                    mine.done(dve.tensor_tensor(a, y, y, ALU.mult))
                    mine.wait()
                    mine.done(dve.scalar_tensor_tensor(out=c, in0=a, scalar=-0.5, in1=var, op0=ALU.mult, op1=ALU.mult))
                    mine.wait()
                    mine.done(dve.scalar_tensor_tensor(out=y, in0=c, scalar=1.5, in1=y, op0=ALU.add, op1=ALU.mult))
                    mine.wait()

            def ln_rows(t0, t1):
                mine.wait()
                for t in range(t0, t1):
                    dve.tensor_scalar(hn[:, t, :], xs[:, t, :], mv[:, t, 0:1], nw[:, 2, t:t + 1],
                                      ALU.subtract, ALU.mult).then_inc(rows_normalised, 1)

            def layernorm(t0, t1, arrived=lambda t: None):
                ln_stats(t0, t1, arrived)
                ln_root(t0, t1)
                ln_rows(t0, t1)

            layernorm(0, TH, lambda t: dve.wait_ge(x_loaded[t // 2], 16))
            dve.wait_ge(consts_loaded, 48)
            for i in range(2):
                dve.tensor_tensor_reduce(lamv[:, 2 * i, :], lamv[:, 2 * i, :], lamv[:, 2 * i + 1, :], 1.0, 0.0,
                                         ALU.mult, ALU.add, lam[:, i:i + 1]).then_inc(lambda_dots, 1)
            dve.wait_ge(lambda_exps, 1)
            mine.done(dve.tensor_tensor(lam[:, 4:5], lam[:, 2:3], lam[:, 3:4], ALU.subtract))
            mine.wait()
            mine.done(dve.tensor_scalar(lam[:, 5:6], lam[:, 4:5], LAMBDA_INIT, None, ALU.add))
            mine.wait()
            dve.tensor_scalar(coef[:], coefc[:, 1:2], lam[:, 5:6], coefc[:, 0:1], ALU.mult, ALU.add).then_inc(coef_ready, 1)
            layernorm(TH, TT, lambda t: dve.wait_ge(x_loaded[2], 16))
            for hf in range(2):
                for n in range(4 * hf, 4 * hf + 4):
                    w, blk = (n % 4) // 2, n % 2
                    high, middle, low = (parts[:, w, j, blk, hf * HALF:(hf + 1) * HALF] for j in range(3))
                    dve.wait_ge(qk_copied, n + 1)
                    dve.wait_ge(qk_high, n + 1)
                    dve.tensor_tensor(qk_rest[:, n % 2, :], qk_f32[:, n % 2, :], high, ALU.subtract).then_inc(qk_left, 1)
                    dve.wait_ge(qk_left, n + 1)
                    mine.done(dve.tensor_copy(middle, qk_rest[:, n % 2, :]))
                    mine.wait()
                    dve.tensor_tensor(low, qk_rest[:, n % 2, :], middle, ALU.subtract).then_inc(qk_low, 1)

            def score_max(n, h, bank):
                dve.wait_ge(scores_ready, n + 1)
                dve.tensor_reduce(row_max[:, :, h:h + 1], bank[:].rearrange("p (t s) -> p t s", t=TB),
                                  AXX, ALU.max).then_inc(scores_used, 1)

            def minus_max(b):
                dve.wait_ge(maxima_turned, b + 1)
                if not (isinstance(b, int) and b == 0):
                    dve.wait_ge(max_rows_out, 16 * b)
                dve.tensor_scalar(minus_max_f[:, 0, :], ps_m[0:2 * H, 0:P], -1.0, None, ALU.mult).then_inc(maxima_read, 1)
                dve.wait_ge(maxima_read, b + 1)
                mine.done(dve.tensor_copy(minus_max_p[:, 0, :], minus_max_f[:, 0, :]))
                mine.wait()
                mine.done(dve.tensor_tensor(minus_max_f[:, 1, :], minus_max_f[:, 0, :], minus_max_p[:, 0, :], ALU.subtract))
                mine.wait()
                mine.done(dve.tensor_copy(minus_max_p[:, 1, :], minus_max_f[:, 1, :]))
                mine.wait()
                dve.tensor_tensor(minus_max_p[:, 2, :], minus_max_f[:, 1, :], minus_max_p[:, 1, :], ALU.subtract).then_inc(minus_max_ready, 1)

            def normalise(b, q):
                dve.wait_ge(quad_turned, 4 * b + q + 5)
                quad = ps_m[:, 0:TB * P].rearrange("p (t j c) -> p t j c", t=TB, j=Q4)
                mine.done(dve.reciprocal(sum_inv[:], quad[:, :, :, HD]))
                mine.wait()
                if q == 0:
                    dve.wait_ge(batch_turned, b + 1)
                dve.tensor_tensor(out_n[:, :, Q4 * q:Q4 * (q + 1), :], quad[:, :, :, 0:HD],
                                  sum_inv[:].unsqueeze(3).broadcast_to([P, TB, Q4, HD]), ALU.mult).then_inc(quad_normalised, 1)

            dve.sem_inc(attention_added, 1)
            for b in range(2):
                for h in range(H):
                    n = H * b + h
                    score_max(n, h, FIRST_S[n % len(FIRST_S)])
                minus_max(b)

            def add_attention(b, tok):
                dve.wait_ge(projected, b + 1)
                dve.scalar_tensor_tensor(out=tok, in0=ps_m[:], scalar=1.0 - LAMBDA_INIT, in1=tok,
                                         op0=ALU.mult, op1=ALU.add).then_inc(attention_added, 1)

            def batch(b, more, tok):
                heads = iter(range(H))

                def maxima(n):
                    if more:
                        for _ in range(n):
                            h = next(heads)
                            score_max(H * b + 2 * H + h, h, ps_s[h % 2])

                for i in range(8):
                    maxima(HEADS_IN_SLOT[i])
                    if i in (3, 5, 7):
                        normalise(b, (i - 3) // 2)
                normalise(b, NQ - 1)
                for n in HEADS_AT_END:
                    maxima(n)
                add_attention(b, tok)
                if more:
                    minus_max(b + 2)

            xflat = xs[:, :, :].rearrange("p t d -> p (t d)")
            def rows_of(b):
                return xflat[:, bass.ds(b * (TB * D), TB * D)]

            per = NQ + 3
            n0 = mine.n
            with dve.Fori(0, 2) as b:
                mine.off = b * per
                batch(b, True, rows_of(b))
            assert mine.n == n0 + per
            mine.off, mine.n = None, n0 + 2 * per
            layernorm(0, TH, lambda t: dve.wait_ge(attention_added, 3))

            def low_hT(stage, hf, banks):
                for k in range(KD):
                    dve.wait_ge(hT_copied, 4 * stage + 2 * hf + k + 1)
                    tok = slice(hf * HALF, (hf + 1) * HALF)
                    dve.tensor_tensor(hTl[:, k, tok], banks[k], hTh[:, k, tok].bitcast(F32), ALU.subtract).then_inc(hT_low, 1)

            def hidden(n):
                dve.wait_ge(voc_silu, n + 1)
                if n >= 2:
                    dve.wait_ge(voc_masked, n - 1)
                dve.tensor_tensor(hidden_f[:, n % 2, :], ps_t[(n % 4) // 2][:, (n % 2) * 512:(n % 2 + 1) * 512],
                                  silu[:, n % 2, :], ALU.mult).then_inc(voc_hidden, 1)

            def hidden_low(n):
                dve.wait_ge(voc_high, n + 1)
                dve.tensor_tensor(voc_Tl[:, n % 8, :], masked[:, n % 4, :], voc_Th[:, n % 8, :].bitcast(F32),
                                  ALU.subtract).then_inc(voc_low, 1)

            def add_experts(t):
                dve.wait_ge(voc_out, t + 1)
                dve.tensor_tensor(xs[:, t, :], ps_s[t % 2][:, 0:D], xs[:, t, :], ALU.add).then_inc(voc_added, 1)

            batch(2, False, rows_of(2))
            dve.wait_ge(masks_ready, 1)
            low_hT(1, 0, (ps_s[0][:], ps_s[1][:]))
            layernorm(TH, TH + TB, lambda t: dve.wait_ge(attention_added, B))
            for q in range(NQ):
                normalise(3, q)
            for n in range(4):
                hidden(n)
                if n >= LOW_LAG:
                    hidden_low(n - LOW_LAG)
            add_attention(3, rows_of(3))
            dve.wait_ge(attention_added, B + 1)
            for n in range(4, 8 + LOW_LAG):
                if n < 8:
                    hidden(n)
                hidden_low(n - LOW_LAG)
                if n in (4, 5, 6):
                    (ln_stats, ln_root, ln_rows)[n - 4](TH + TB, TT)
            for t in range(2):
                add_experts(t)
            low_hT(1, 1, (ps_o[:], ps_m[:]))
            for t in range(2, TH):
                add_experts(t)
            dve.wait_ge(voc_added, TH)
            for n in range(8, 16 + LOW_LAG):
                if n < 16:
                    hidden(n)
                if n >= 8 + LOW_LAG:
                    hidden_low(n - LOW_LAG)
                if n in (9, 11, 13):
                    (ln_stats, ln_root, ln_rows)[(n - 9) // 2](0, TH)
            for t in range(TH, TH + 2):
                add_experts(t)
            low_hT(2, 0, (ps_o[:], ps_m[:]))
            dve.wait_ge(voc_added, TH + 2)
            layernorm(TH, TH + 2)
            for t in range(TH + 2, TT):
                add_experts(t)
            dve.wait_ge(voc_added, TT)
            layernorm(TH + 2, TT)

            def shared_mult(hf, fs):
                for f in fs:
                    m = FS * hf + f
                    dve.wait_ge(shared_silu, m + 1)
                    if hf == 1:
                        dve.wait_ge(shared_out, TH)
                    dve.tensor_tensor(shared_T[:, f, :], ps_t[m % 2][:, 512:1024], silu[:, m % 2, :], ALU.mult).then_inc(shared_units, 1)

            shared_mult(0, range(0, 3))
            low_hT(2, 1, (ps_o[:], ps_m[:]))
            shared_mult(0, range(3, 4))
            dve.wait_ge(logits_turned, 1)
            mine.done(dve.tensor_copy(logits[:], ps_o[:, 0:TT * E].rearrange("p (t e) -> p t e", t=TT)))
            mine.wait()
            for t in range(TT):
                mine.done(dve.max(top8[:, t, :], logits[:, t, :]))
            mine.wait()
            for t in range(TT):
                mine.done(dve.max_index(top8_at[:, t, :], top8[:, t, :], logits[:, t, :]))
            dve.tensor_tensor(gates[:, 0, :], top8[:, :, 1], top8[:, :, 0], ALU.subtract).then_inc(gate_difference, 1)
            mine.wait()
            mine.done(dve.tensor_copy(top2_at[:], top8_at[:, :, 0:2]))
            mine.wait()
            for r in range(2):
                mine.done(dve.tensor_tensor(onehot[:, r, :, :], iota[:].unsqueeze(1).broadcast_to([P, TT, E]),
                                            top2_at[:, :, r:r + 1].broadcast_to([P, TT, E]), ALU.is_equal))
            mine.wait()
            dve.tensor_tensor(chosen[:], onehot[:, 0, :, :], onehot[:, 1, :, :], ALU.add).then_inc(chosen_ready, 1)
            def shared_add(tiles_of):
                for t in tiles_of:
                    dve.wait_ge(shared_out, t + 1)
                    dve.tensor_tensor(xs[:, t, :], ps_s[t % 2][:, 0:D], xs[:, t, :], ALU.add).then_inc(shared_added, 1)

            shared_mult(0, range(4, 6))
            dve.wait_ge(ranks_ready, 1)
            dve.wait_ge(counting_loaded, 32)
            n_i, n_t, n_f, ends, starts, ones8 = (cnt[:, i, :] for i in range(6))
            mine.done(dve.tensor_scalar(n_i.bitcast(I32), ps_m[:, TT * E:TT * E + E], float(P - 1), None, ALU.add))
            mine.done(dve.memset(ones8, 1.0))
            mine.wait()
            mine.done(dve.tensor_scalar(n_t.bitcast(I32), n_i.bitcast(I32), 7, None, ALU.logical_shift_right))
            mine.wait()
            mine.done(dve.tensor_copy(n_f, n_t.bitcast(I32)))
            mine.wait()
            mine.done(dve.tensor_tensor_scan(ends, ones8, n_f, 0.0, ALU.mult, ALU.add))
            mine.wait()
            mine.done(dve.tensor_tensor(starts, ends, n_f, ALU.subtract))
            mine.done(dve.tensor_tensor(tile_ge[:], tiles[:], ends[0:1, 0:E - 1].unsqueeze(1).broadcast_to([1, NM, E - 1]), ALU.is_ge))
            mine.wait()
            mine.done(dve.scalar_tensor_tensor(out=posf[:], in0=starts.unsqueeze(1).broadcast_to([P, TT, E]),
                                               scalar=float(P), in1=ps_m[:, 0:TT * E].rearrange("p (t e) -> p t e", t=TT),
                                               op0=ALU.mult, op1=ALU.add))
            mine.done(dve.tensor_reduce(eidf[:], tile_ge[:], AXX, ALU.add))
            mine.wait()
            dve.tensor_copy(eid[:], eidf[:]).then_inc(tile_experts_ready, 1)
            for r in range(2):
                mine.done(dve.tensor_tensor(posm[:, r, :, :], onehot[:, r, :, :], posf[:], ALU.mult))
            mine.wait()
            mine.done(dve.tensor_reduce(posr[:], posm[:], AXX, ALU.add))
            mine.wait()
            dve.tensor_copy(pos[:], posr[:].rearrange("p r t -> p (r t)")).then_inc(places_ready, 1)
            dve.wait_ge(gate_exp, 1)
            mine.done(dve.tensor_scalar(gates[:, 2, :], gates[:, 1, :], 1.0, None, ALU.add))
            mine.wait()
            mine.done(dve.reciprocal(gates[:, 3, :], gates[:, 2, :]))
            mine.wait()
            mine.done(dve.tensor_tensor(gates[:, 0, :], gates[:, 3, :], gates[:, 1, :], ALU.mult))
            shared_mult(0, range(6, FS))
            shared_add(range(TH))
            shared_mult(1, range(0, FS // 2))
            dve.sem_inc(tile_units, 2)
            dve.sem_inc(tile_down_copied, 2)

            def tile_mult(i, par):
                dve.wait_ge(tile_gate_silu, i + 1)
                dve.wait_ge(tile_ups, i + 3)
                dve.wait_ge(units_turned, i + 1)
                dve.tensor_tensor(units[:, par, :], ps_t[par][:, 512:1024], tile_silu_sb[:, par, :], ALU.mult).then_inc(tile_units, 1)

            def tile_out(i, par, stored):
                dve.wait_ge(tile_down, i + 3)
                if stored is not None:
                    dve.wait_ge(tile_stored[par], stored)
                dve.tensor_copy(tile_y[:, par, :], ps_s[par][:, 0:D]).then_inc(tile_down_copied, 1)

            tile_mult(0, 0)
            tile_mult(1, 1)
            tile_out(0, 0, None)
            tile_mult(2, 0)
            tile_out(1, 1, None)
            with dve.Fori(1, NM // 2) as j:
                for par in range(2):
                    i = 2 * j + par
                    tile_mult(i + 1, 1 - par)
                    tile_out(i, par, 16 * j)
            tile_out(NM - 1, 0, 16 * (NM // 2))
            shared_mult(1, range(FS // 2, FS))

            def combine(t):
                mine.done(dve.scalar_tensor_tensor(out=xs[:, t, :], in0=gathered[:, 0, t, :], scalar=gates[:, 3, t:t + 1],
                                                   in1=xs[:, t, :], op0=ALU.mult, op1=ALU.add))
                mine.wait()
                return dve.scalar_tensor_tensor(out=xs[:, t, :], in0=gathered[:, 1, t, :], scalar=gates[:, 0, t:t + 1],
                                                in1=xs[:, t, :], op0=ALU.mult, op1=ALU.add)

            dve.wait_ge(shared_added, TH)
            dve.wait_ge(rows_gathered[0], 32 * TH)
            for t in range(TH):
                combine(t).then_inc(rows_final, 1)
            shared_add(range(TH, TT - 1))
            dve.wait_ge(rows_gathered[1], 32 * TH)
            dve.wait_ge(shared_added, TT - 1)
            for t in range(TH, TT - 1):
                combine(t).then_inc(rows_final, 1)
            mine.done(combine(TT - 1))
            mine.wait()
            dve.wait_ge(shared_out, TT)
            dve.tensor_tensor(xs[:, TT - 1, :], ps_s[(TT - 1) % 2][:, 0:D], xs[:, TT - 1, :], ALU.add).then_inc(rows_final, 1)

        @block.tensor
        def _(pe):
            def transposes(stage, hf, banks):
                for k in range(KD):
                    pe.wait_ge(rows_normalised, 8 * stage + TH * (hf + 1))
                    n = 4 * stage + 2 * hf + k
                    if n >= 2:
                        pe.wait_ge(hT_copied, n - 1)
                    if n >= 6:
                        pe.wait_ge(hT_low, n - 5)
                    for t in range(TH):
                        last = pe.transpose(banks[k][:, t * P:(t + 1) * P], hn[:, hf * TH + t, k * P:(k + 1) * P], ident[:])
                    last.then_inc(hT_product, 1)

            pe.sem_inc(weighted_done, 2)
            pe.sem_inc(tile_turned, 2)
            pe.sem_inc(tile_ups, 2)
            pe.sem_inc(tile_down, 2)
            pe.sem_inc(units_turned, 2)

            pe.wait_ge(ident_loaded, 16)
            for _ in range(WARM_UP):
                pe.matmul(ps_t[0][:, 0:512], ident[:], ident[:].unsqueeze(1).broadcast_to([P, 4, P]), start=True, stop=True)
            pe.wait_ge(wqk_loaded, 16)
            for hf in range(2):
                tok = slice(hf * HALF, (hf + 1) * HALF)
                transposes(0, hf, ps_s)
                pe.wait_ge(hT_copied, 2 * hf + 2)
                for n in range(4 * hf, 4 * hf + 4):
                    if hf == 1:
                        pe.wait_ge(qk_high, n - 3)
                    bank = ps_t[(n % 4) // 2][:, (n % 2) * 512:(n % 2 + 1) * 512]
                    for k in range(KD):
                        last = pe.matmul(bank, w_qk_sb[:, k, (n % 4) * P:(n % 4 + 1) * P], hT[:, k, tok],
                                         start=(k == 0), stop=(k == KD - 1))
                    last.then_inc(qk_product, 1)
                if hf == 0:
                    pe.wait_ge(wv_loaded, 16)
                for i, bank in enumerate((ps_o, ps_m)):
                    if hf == 1:
                        pe.wait_ge(v_copied, i + 1)
                    for t in range(2):
                        tt = hf * TH + 2 * i + t
                        for k in range(KD):
                            last = pe.matmul(bank[:, t * D:(t + 1) * D], hT[:, k, tt * P:(tt + 1) * P], w_v_sb[:, k, :],
                                             start=(k == 0), stop=(k == KD - 1))
                    last.then_inc(v_product, 1)

            def scores(bank, h, rows, keys):
                for tt in range(TB):
                    last = pe.matmul(bank[:, tt * S:(tt + 1) * S], rows(h, tt), keys(h), start=True, stop=True)
                last.then_inc(scores_ready, 1)

            def rows_of(b):
                return (lambda h, tt: q_rows[0:KS_ROWS, h, bass.ds(b * S + tt * P, P)],
                        lambda h: k_rows[0:KS_ROWS, h, bass.ds(b * S, S)])

            def max_rows(b):
                pe.wait_ge(scores_used, H * b + H + 2)
                pe.transpose(ps_m[0:2 * H, 0:P], row_max[:, :, :].rearrange("p t h -> p (t h)"), ident[:]).then_inc(maxima_turned, 1)

            def exps_in(b, i):
                q, st = i // 2, i % 2
                if i == 0:
                    pe.wait_ge(max_rows_in, 32 * b + 32)
                pe.wait_ge(weights_ready, 8 * b + i + 1)
                for j in range(Q4):
                    h = Q4 * q + j
                    last = pe.matmul(ps_t[i % 2][:, j * S:(j + 1) * S], k_rows[0:KA_ROWS, h, bass.ds(b * S + st * P, P)],
                                     q_rows[0:KA_ROWS, h, bass.ds(b * S, S)], start=True, stop=True)
                last.then_inc(exponents_ready, 1)

            def batch(b, more, following, fill=lambda n: None):
                heads = iter(range(H))
                if more:
                    rows, keys = rows_of(b + 2)

                def maxima(n):
                    if more:
                        for _ in range(n):
                            h = next(heads)
                            pe.wait_ge(scores_used, H * b + 2 * H + h + 1)
                            scores(ps_s[h % 2], h, rows, keys)

                def values(i):
                    q, st = i // 2, i % 2
                    pe.wait_ge(weights_ready, 8 * b + i + 3)
                    if i == 0:
                        pe.wait_ge(values_ready, b + 1)
                    if st == 0:
                        pe.wait_ge(out_copied, 4 * b + q + 1)
                    for j in range(Q4):
                        h = Q4 * q + j
                        last = pe.matmul(ps_o[HP * j:HP * (j + 1), 0:S], values_1[:, st, h, :], probs[:, i % 2, j * S:(j + 1) * S],
                                         start=(st == 0), stop=(st == TB - 1))
                    last.then_inc(weighted_done, 1)

                def turn_quad(q):
                    pe.wait_ge(out_copied, 4 * b + q + 2)
                    if q == 0:
                        pe.wait_ge(attention_added, b + 1)
                        pe.wait_ge(maxima_read, b + 2 if more else B)
                    else:
                        pe.wait_ge(quad_normalised, 4 * b + q)
                    for tt in range(TB):
                        last = pe.transpose(ps_m[:, tt * P:(tt + 1) * P], out_sb[:, q, tt * P:(tt + 1) * P], ident[:])
                    last.then_inc(quad_turned, 1)

                for i in range(8):
                    if 0 < i < 7:
                        exps_in(b, i + 1)
                    elif i == 7 and following:
                        exps_in(b + 1, 0)
                    maxima(HEADS_IN_SLOT[i])
                    values(i)
                    if i in (3, 5, 7):
                        turn_quad((i - 3) // 2)
                turn_quad(NQ - 1)
                if following:
                    exps_in(b + 1, 1)
                for n in range(2):
                    fill(n)
                maxima(HEADS_AT_END[0])
                pe.wait_ge(quad_normalised, 4 * b + 4)
                for tt in range(TB):
                    rows_n = out_n[:, tt, :, :].rearrange("p h d -> p (h d)")
                    for k in range(KD):
                        last = pe.transpose(ps_m[:, (KD * tt + k) * P:(KD * tt + k + 1) * P], rows_n[:, k * P:(k + 1) * P],
                                            ident[:])
                last.then_inc(batch_turned, 1)
                maxima(HEADS_AT_END[1])
                for n in range(2, 4):
                    fill(n)
                pe.wait_ge(batch_copied, b + 1)
                for tt in range(TB):
                    for k in range(KD):
                        last = pe.matmul(ps_m[:, tt * D:(tt + 1) * D], out_T[:, tt, k, :], w_proj_sb[:, k, :],
                                         start=(k == 0), stop=(k == KD - 1))
                last.then_inc(projected, 1)
                if more:
                    pe.wait_ge(attention_added, b + 2)
                    max_rows(b + 2)

            pe.sem_inc(quad_turned, NQ)
            pe.sem_inc(batch_turned, 1)
            pe.wait_ge(v_copied, 4)
            for b in range(2):
                pe.wait_ge(qk_parts_in[b], 192)
                rows, keys = rows_of(b)
                for h in range(H):
                    n = H * b + h
                    if n >= len(FIRST_S):
                        pe.wait_ge(scores_used, n + 3 - len(FIRST_S))
                    scores(FIRST_S[n % len(FIRST_S)], h, rows, keys)
                if b == 1:
                    pe.wait_ge(maxima_read, 1)
                max_rows(b)
            pe.wait_ge(qk_parts_in[2], 192)
            pe.wait_ge(qk_high, 8)
            pe.wait_ge(memsets_done, 2)
            pe.wait_ge(wproj_loaded, 16)
            for i in range(2):
                exps_in(0, i)
            with pe.Fori(0, 2) as b:
                batch(b, True, True)
            batch(2, False, True)
            pe.wait_ge(scores_used, H * B + 2)
            transposes(1, 0, ps_s)
            def experts_up(n):
                hf, e, fb = n // 8, (n % 8) // 2, n % 2
                if n == 0:
                    pe.wait_ge(ctx_split, 2)
                    pe.wait_ge(hT_low, 2)
                    pe.wait_ge(weights_ready, 8 * B + 2)
                if n >= 4:
                    pe.wait_ge(voc_hidden, n - 3)
                if n == 8:
                    pe.wait_ge(hT_low, 4)
                bank = ps_t[(n % 4) // 2][:, (n % 2) * 512:(n % 2 + 1) * 512]
                w, tok = slice(fb * P, (fb + 1) * P), slice(hf * HALF, (hf + 1) * HALF)
                terms = [(u[:, e, k, w], v[:, k, tok]) for k in range(KD) for u, v in ((ctx_h, hTh), (ctx_h, hTl), (ctx_l, hTh))]
                for j, (u, v) in enumerate(terms):
                    last = pe.matmul(bank, u, v, start=(j == 0), stop=(j == len(terms) - 1))
                last.then_inc(voc_product, 1)

            def experts_down(hf, i, ts):
                pe.wait_ge(voc_low, 8 * hf + i + 1)
                for t in ts:
                    if i == 0 and hf * TH + t >= 2:
                        pe.wait_ge(voc_added, hf * TH + t - 1)
                    rows = slice(t * P, (t + 1) * P)
                    for j, (u, v) in enumerate(((voc_Th, ctx_h), (voc_Th, ctx_l), (voc_Tl, ctx_h))):
                        last = pe.matmul(ps_s[t % 2][:, 0:D], u[:, i, rows], v[:, i // 2, i % 2, :],
                                         start=(i == 0 and j == 0), stop=(i == XE * KD - 1 and j == 2))
                    if i == XE * KD - 1:
                        last.then_inc(voc_out, 1)

            batch(3, False, False, experts_up)
            for hf in range(2):
                for i in range((4, 0)[hf], 8 + DOWN_LAG):
                    if i < 8:
                        experts_up(8 * hf + i)
                    if i >= DOWN_LAG:
                        experts_down(hf, i - DOWN_LAG, (0, 1))
                transposes(1 + hf, 1 - hf, (ps_o, ps_m))
                for t in (2, 3):
                    for i in range(8):
                        experts_down(hf, i, (t,))

            def shared_up(hf, fs):
                tok = slice(hf * HALF, (hf + 1) * HALF)
                for f in fs:
                    m = FS * hf + f
                    if m >= 2:
                        pe.wait_ge(shared_units, m - 1)
                    pe.wait_ge(shared_w_low, f // 4 + 1)
                    high, fh, fw = shared_gu_h[f // 4], slice(f % 4 * P, (f % 4 + 1) * P), slice(f * P, (f + 1) * P)
                    for o in range(2):
                        for k in range(KD):
                            terms = ((high[:, o, k, fh], hTh), (high[:, o, k, fh], hTl), (shared_gu_l[:, o, k, fw], hTh))
                            for j, (u, v) in enumerate(terms):
                                last = pe.matmul(ps_t[m % 2][:, o * 512:(o + 1) * 512], u, v[:, k, tok],
                                                 start=(k == 0 and j == 0), stop=(k == KD - 1 and j == 2))
                    last.then_inc(shared_product, 1)

            def shared_down(hf):
                for t in range(TH):
                    tt = hf * TH + t
                    if t >= 2:
                        pe.wait_ge(shared_added, tt - 1)
                    for f in range(FS):
                        if t == 0:
                            pe.wait_ge(shared_units, FS * hf + f + 1)
                        last = pe.matmul(ps_s[tt % 2][:, 0:D], shared_T[:, f, t * P:(t + 1) * P], shared_d[:, f, :],
                                         start=(f == 0), stop=(f == FS - 1))
                    last.then_inc(shared_out, 1)

            pe.wait_ge(voc_hidden, 16)
            pe.wait_ge(shared_w_loaded, 48)
            pe.wait_ge(hT_low, 6)
            shared_up(0, range(0, 3))
            transposes(2, 1, (ps_o, ps_m))
            pe.wait_ge(router_split, 2)
            pe.wait_ge(hT_low, 8)
            for hf, bank in enumerate((ps_o, ps_m)):
                tok = slice(hf * HALF, (hf + 1) * HALF)
                terms = [(u[:, k, :], v[:, k, tok]) for k in range(KD) for u, v in ((router_h, hTh), (router_h, hTl), (router_l, hTh))]
                for j, (u, v) in enumerate(terms):
                    last = pe.matmul(bank[0:E, :], u, v, start=(j == 0), stop=(j == len(terms) - 1))
                last.then_inc(logits_product, 1)
            shared_up(0, range(3, 4))
            pe.wait_ge(logits_copied, 2)
            for tt in range(TT):
                last = pe.transpose(ps_o[:, tt * E:(tt + 1) * E], logitsT[:, tt * P:(tt + 1) * P], ident[0:E, 0:E])
            last.then_inc(logits_turned, 1)
            shared_up(0, range(4, 6))
            pe.wait_ge(chosen_ready, 1)
            pe.wait_ge(counting_ready, 2)
            pe.matmul(ps_m[:, 0:TT * E], beforeb[:], chosen[:].rearrange("p t e -> p (t e)"), start=True, stop=False,
                      skip_group_check=True)
            for t in range(TT - 1):
                later = TT - 1 - t
                pe.matmul(ps_m[:, (t + 1) * E:TT * E], onesb[:], chosen[:, t:t + 1, :].broadcast_to([P, later, E]),
                          start=False, stop=False, skip_group_check=True)
            for t in range(TT):
                last = pe.matmul(ps_m[:, TT * E:TT * E + E], onesb[:], chosen[:, t, :], start=False, stop=(t == TT - 1),
                                 skip_group_check=True)
            last.then_inc(ranks_ready, 1)
            shared_up(0, range(6, FS))
            shared_down(0)
            shared_up(1, range(0, FS // 2 - 1))

            def expert_of(i):
                return pe.value_load(eid[0:1, bass.ds(i, 1)], min_val=0, max_val=E - 1)

            def turn_rows(i, par, loads):
                pe.wait_ge(tile_loaded[par], loads)
                pe.wait_ge(tile_copied, i) if not isinstance(i, int) or i > 0 else None
                for k in range(KD):
                    last = pe.transpose(ps_o[:, k * P:(k + 1) * P], tile_x[:, par, k * P:(k + 1) * P], ident[:])
                last.then_inc(tile_turned, 1)

            def up(i, par):
                e = expert_of(i)
                pe.wait_ge(tile_copied, i + 1)
                pe.wait_ge(tile_units, i + 1)
                for o, done in ((0, tile_gates), (1, tile_ups)):
                    for k in range(KD):
                        last = pe.matmul(ps_t[par][:, o * 512:(o + 1) * 512], tile_xT[:, par, k * P:(k + 1) * P],
                                         big_place[:, bass.ds(e * W1S + (2 * k + o) * INTER, INTER)],
                                         start=(k == 0), stop=(k == KD - 1))
                    last.then_inc(done, 1)

            def turn_hidden(i, par):
                pe.wait_ge(tile_units, i + 3)
                pe.wait_ge(units_copied, i) if not isinstance(i, int) or i > 0 else None
                for f in range(FB):
                    last = pe.transpose(ps_m[:, f * P:(f + 1) * P], units[:, par, f * P:(f + 1) * P], ident[:])
                last.then_inc(units_turned, 1)

            def down(i, par):
                e = expert_of(i)
                pe.wait_ge(units_copied, i + 1)
                pe.wait_ge(tile_down_copied, i + 1)
                for f in range(FB):
                    last = pe.matmul(ps_s[par][:, 0:D], unitsT[:, par, f * P:(f + 1) * P],
                                     big_place[:, bass.ds(e * W2S + W2O + f * D, D)], start=(f == 0), stop=(f == FB - 1))
                last.then_inc(tile_down, 1)

            turn_rows(0, 0, 16)
            shared_up(1, range(FS // 2 - 1, FS // 2))
            pe.wait_ge(tile_experts_ready, 1)
            pe.wait_ge(expert_w_loaded, 16 * 2 * E)
            pe.wait_ge(shared_added, TH)
            pe.wait_ge(shared_units, FS + FS // 2 - 1)
            up(0, 0)
            pe.wait_ge(shared_units, FS + FS // 2)
            with pe.Fori(0, NM // 2) as j:
                for par in range(2):
                    i = 2 * j + par
                    turn_rows(i + 1, 1 - par, 16 * j + 16 * (par + 1))
                    turn_hidden(i, par)
                    up(i + 1, 1 - par)
                    down(i, par)
            turn_hidden(NM - 1, 0)
            down(NM - 1, 0)
            pe.wait_ge(tile_units, NM + 2)
            pe.wait_ge(tile_down_copied, NM + 2)
            shared_up(1, range(FS // 2, FS))
            shared_down(1)


def _consts():
    p = np.arange(P)
    ident = np.eye(P, dtype=np.float32)
    first = (p % HD) < HD // 2
    coef = np.stack([np.where(first, SCALE, 0.0), np.where(first, 0.0, -SCALE)], axis=1).astype(np.float32)
    iota = np.tile(np.arange(E, dtype=np.float32), (P, 1))
    before = (p[:, None] < p[None, :]).astype(np.float32)
    tiles = np.repeat(np.arange(NM, dtype=np.float32)[:, None], E - 1, axis=1)[None]
    return {"ident": ident, "coef": coef, "iota": iota, "before": before, "tiles": tiles}


def kernel(x, itok_BxS_13_99985, ctx_2048, L0_attn_W_attn, L0_attn_W_proj, L0_attn_lambda_q1, L0_attn_lambda_k1,
           L0_attn_lambda_q2, L0_attn_lambda_k2, L0_ffn_router_w, L0_ffn_w1, L0_ffn_w2, L0_ffn_w_gate, L0_ffn_w_up,
           L0_ffn_w_down):
    import concourse.bacc as _bacc
    from concourse.bass_utils import run_bass_kernel_spmd as _run

    C = D // 2
    w = np.asarray(L0_attn_W_attn)
    q1, k1, q2, k2 = (w[:, i * C:(i + 1) * C].reshape(D, H, HD // 2) for i in range(4))
    wq = np.concatenate([q1, q2], axis=2).reshape(D, D)
    wk = np.concatenate([k1, k2], axis=2).reshape(D, D)
    w_qk_sb = np.concatenate([wq, wk], axis=1).reshape(KD, P, 2 * D).transpose(1, 0, 2)
    w_v_sb = w[:, 4 * C:].reshape(KD, P, D).transpose(1, 0, 2)
    w_proj_sb = np.asarray(L0_attn_W_proj).reshape(KD, P, D).transpose(1, 0, 2)
    ctxT = np.asarray(ctx_2048).transpose(2, 0, 1).reshape(KD, P, XE, D).transpose(1, 2, 0, 3)
    lam_vecs = np.stack([np.asarray(L0_attn_lambda_q1), np.asarray(L0_attn_lambda_k1),
                         np.asarray(L0_attn_lambda_q2), np.asarray(L0_attn_lambda_k2)])
    c = _consts()
    arrays = {
        "x": x, "ids": np.asarray(itok_BxS_13_99985).reshape(T), "ctxT": ctxT, "w_qk": w_qk_sb, "w_v": w_v_sb, "w_proj": w_proj_sb,
        "lam_vecs": lam_vecs, "router_w": L0_ffn_router_w, "w1": L0_ffn_w1, "w2": L0_ffn_w2,
        "w_gate": L0_ffn_w_gate, "w_up": L0_ffn_w_up, "w_down": L0_ffn_w_down,
        "ident_c": c["ident"], "coef_c": c["coef"], "iota_c": c["iota"],
        "before_c": c["before"], "tiles_c": c["tiles"],
    }
    nc = _bacc.Bacc("TRN2", target_bir_lowering=False, num_devices=1)
    feeds, args = {}, []
    for name, a in arrays.items():
        a = np.ascontiguousarray(a)
        feeds[f"in_{name}"] = a
        args.append(nc.dram_tensor(f"in_{name}", a.shape, mybir.dt.from_np(a.dtype), kind="ExternalInput").ap())
    args.append(nc.dram_tensor("out_0", (B, S, D), F32, kind="ExternalOutput").ap())
    decoder_layer(nc, *args)
    r = _run(nc, [feeds], core_ids=[0])
    return r.results[0]["out_0"]
```
